# Optimizing a Trainium2 kernel written in Bass

```python
import numpy as np
import jax
import jax.numpy as jnp

def _softmax(x, axis=-1):
    return jax.nn.softmax(x, axis=axis)

def _gelu(x):
    return jax.nn.gelu(x, approximate=True)

def _silu(x):
    return jax.nn.silu(x)

def _sigmoid(x):
    return jax.nn.sigmoid(x)

def _layernorm(x, axis=-1, eps=1e-05):
    m = jnp.mean(x, axis=axis, keepdims=True)
    v = jnp.var(x, axis=axis, keepdims=True)
    return (x - m) / jnp.sqrt(v + eps)

def _scatter_add(tgt, idx, src, axis=0):
    return tgt.at[idx].add(src)

def _segment_sum(src, seg, n):
    return jax.ops.segment_sum(src, seg, n)
kernel_name = 'mk_sandwich_d1_jaxref_r4_adb6c4'

def setup_inputs(seed: int=0):
    np.random.seed(seed)
    _w = jnp.asarray

    def _L0_attn_setup():
        import jax, jax.numpy as jnp
        import numpy as np
        N_HEADS = 16
        BUCKETS = 64
        MAX_REL = 128
        ATT_SPAN = BUCKETS
        LN_EPS = 1e-07

        def make_log_bucket_position(relative_pos, bucket_size, max_position):
            sign = jnp.sign(relative_pos)
            mid = bucket_size // 2
            abs_pos = jnp.where((relative_pos < mid) & (relative_pos > -mid), mid - 1, jnp.abs(relative_pos))
            log_pos = jnp.ceil(jnp.log(abs_pos / mid) / jnp.log((max_position - 1) / mid) * (mid - 1)) + mid
            bucket_pos = jnp.where(abs_pos <= mid, abs_pos, log_pos * sign)
            return bucket_pos.astype(jnp.int32)

        def build_relative_position(q_size, k_size, bucket_size, max_position):
            rel = jnp.arange(q_size)[:, None] - jnp.arange(k_size)[None, :]
            rel = make_log_bucket_position(rel, bucket_size, max_position)
            return rel.astype(jnp.int32)
        key = jax.random.key(seed)
        ks = jax.random.split(key, 16)
        B, S, H = (4, 256, 256)
        std = 0.02
        inp = {'hidden_states': jax.random.normal(ks[0], (B, S, H), jnp.float32), 'attention_mask': jnp.ones((B, S), jnp.float32), 'rel_embeddings': jax.random.normal(ks[1], (2 * ATT_SPAN, H), jnp.float32) * std, 'Wq': jax.random.normal(ks[2], (H, H), jnp.float32) * std, 'bq': jnp.zeros((H,), jnp.float32), 'Wk': jax.random.normal(ks[3], (H, H), jnp.float32) * std, 'bk': jnp.zeros((H,), jnp.float32), 'Wv': jax.random.normal(ks[4], (H, H), jnp.float32) * std, 'bv': jnp.zeros((H,), jnp.float32), 'Wo': jax.random.normal(ks[5], (H, H), jnp.float32) * std, 'bo': jnp.zeros((H,), jnp.float32), 'ln_scale': jnp.ones((H,), jnp.float32), 'ln_bias': jnp.zeros((H,), jnp.float32)}
        return inp
    _L0_attn_in = _L0_attn_setup()

    def _L0_ffn_setup():
        import jax, jax.numpy as jnp
        import numpy as np
        E, D, H = (8, 256, 1024)
        B, S = (4, 1024)
        TEMPERATURE = 1.0
        key = jax.random.key(seed)
        ks = jax.random.split(key, 7)
        sc = 0.02
        return {'x': jax.random.normal(ks[0], (B, S, D), dtype=jnp.float32), 'W1': jax.random.normal(ks[1], (E, D, H), dtype=jnp.float32) * sc, 'b1': jax.random.normal(ks[2], (E, H), dtype=jnp.float32) * sc, 'W2': jax.random.normal(ks[3], (E, H, D), dtype=jnp.float32) * sc, 'b2': jax.random.normal(ks[4], (E, D), dtype=jnp.float32) * sc, 'Wr': jax.random.normal(ks[5], (D, E), dtype=jnp.float32) * sc, 'br': jax.random.normal(ks[6], (E,), dtype=jnp.float32) * sc}
    _L0_ffn_in = _L0_ffn_setup()
    _d = {'L0_attn_hidden_states': _L0_attn_in['hidden_states'], 'L0_attn_attention_mask': _L0_attn_in['attention_mask'], 'L0_attn_rel_embeddings': _L0_attn_in['rel_embeddings'], 'L0_attn_Wq': _L0_attn_in['Wq'], 'L0_attn_bq': _L0_attn_in['bq'], 'L0_attn_Wk': _L0_attn_in['Wk'], 'L0_attn_bk': _L0_attn_in['bk'], 'L0_attn_Wv': _L0_attn_in['Wv'], 'L0_attn_bv': _L0_attn_in['bv'], 'L0_attn_Wo': _L0_attn_in['Wo'], 'L0_attn_bo': _L0_attn_in['bo'], 'L0_attn_ln_scale': _L0_attn_in['ln_scale'], 'L0_attn_ln_bias': _L0_attn_in['ln_bias'], 'L0_ffn_W1': _L0_ffn_in['W1'], 'L0_ffn_b1': _L0_ffn_in['b1'], 'L0_ffn_W2': _L0_ffn_in['W2'], 'L0_ffn_b2': _L0_ffn_in['b2'], 'L0_ffn_Wr': _L0_ffn_in['Wr'], 'L0_ffn_br': _L0_ffn_in['br']}
    _x0 = _d['L0_attn_hidden_states']
    _d['L0_attn_hidden_states'] = jax.random.normal(jax.random.fold_in(jax.random.key(seed), 1), (4, 1024, 256), dtype=_x0.dtype)
    del _x0
    return _d

def reference(L0_attn_hidden_states, L0_attn_attention_mask, L0_attn_rel_embeddings, L0_attn_Wq, L0_attn_bq, L0_attn_Wk, L0_attn_bk, L0_attn_Wv, L0_attn_bv, L0_attn_Wo, L0_attn_bo, L0_attn_ln_scale, L0_attn_ln_bias, L0_ffn_W1, L0_ffn_b1, L0_ffn_W2, L0_ffn_b2, L0_ffn_Wr, L0_ffn_br):

    def _L0_attn_ref(hidden_states, attention_mask, rel_embeddings, Wq, bq, Wk, bk, Wv, bv, Wo, bo, ln_scale, ln_bias):
        import jax, jax.numpy as jnp
        import numpy as np
        N_HEADS = 16
        BUCKETS = 64
        MAX_REL = 128
        ATT_SPAN = BUCKETS
        LN_EPS = 1e-07

        def make_log_bucket_position(relative_pos, bucket_size, max_position):
            sign = jnp.sign(relative_pos)
            mid = bucket_size // 2
            abs_pos = jnp.where((relative_pos < mid) & (relative_pos > -mid), mid - 1, jnp.abs(relative_pos))
            log_pos = jnp.ceil(jnp.log(abs_pos / mid) / jnp.log((max_position - 1) / mid) * (mid - 1)) + mid
            bucket_pos = jnp.where(abs_pos <= mid, abs_pos, log_pos * sign)
            return bucket_pos.astype(jnp.int32)

        def build_relative_position(q_size, k_size, bucket_size, max_position):
            rel = jnp.arange(q_size)[:, None] - jnp.arange(k_size)[None, :]
            rel = make_log_bucket_position(rel, bucket_size, max_position)
            return rel.astype(jnp.int32)
        B, S, H = hidden_states.shape
        nH = N_HEADS
        d = H // nH

        def split_heads(x):
            return jnp.transpose(x.reshape(B, S, nH, d), (0, 2, 1, 3))
        q = split_heads(hidden_states @ Wq + bq)
        k = split_heads(hidden_states @ Wk + bk)
        v = split_heads(hidden_states @ Wv + bv)
        scale_factor = 3
        scale = jnp.sqrt(jnp.asarray(d * scale_factor, hidden_states.dtype))
        scores = jnp.einsum('bhqd,bhkd->bhqk', q, k) / scale
        rel = build_relative_position(S, S, BUCKETS, MAX_REL)
        pos_k = (rel_embeddings @ Wk + bk).reshape(2 * ATT_SPAN, nH, d)
        pos_k = jnp.transpose(pos_k, (1, 0, 2))
        c2p_att = jnp.einsum('bhqd,hpd->bhqp', q, pos_k)
        c2p_pos = jnp.clip(rel + ATT_SPAN, 0, 2 * ATT_SPAN - 1)
        c2p = jnp.take_along_axis(c2p_att, jnp.broadcast_to(c2p_pos[None, None], (B, nH, S, S)), axis=-1)
        p2c_pos = jnp.clip(-rel + ATT_SPAN, 0, 2 * ATT_SPAN - 1)
        p2c_att = jnp.einsum('bhkd,hpd->bhkp', k, pos_k)
        p2c = jnp.take_along_axis(p2c_att, jnp.broadcast_to(p2c_pos[None, None], (B, nH, S, S)), axis=-1)
        p2c = jnp.swapaxes(p2c, -1, -2)
        scores = scores + (c2p + p2c) / scale
        probs = jax.nn.softmax(scores, axis=-1)
        ctx = jnp.einsum('bhqk,bhkd->bhqd', probs, v)
        ctx = jnp.transpose(ctx, (0, 2, 1, 3)).reshape(B, S, H)
        out = ctx @ Wo + bo + hidden_states
        mu = jnp.mean(out, axis=-1, keepdims=True)
        var = jnp.mean(jnp.square(out - mu), axis=-1, keepdims=True)
        out = (out - mu) * jax.lax.rsqrt(var + LN_EPS) * ln_scale + ln_bias
        return out

    def _L0_ffn_ref(x, W1, b1, W2, b2, Wr, br):
        import jax, jax.numpy as jnp
        import numpy as np
        E, D, H = (8, 256, 1024)
        B, S = (4, 1024)
        TEMPERATURE = 1.0
        routing_logits = (x @ Wr + br) / TEMPERATURE
        routing_probs = jax.nn.softmax(routing_logits, axis=-1)
        indices = jnp.argmax(routing_probs, axis=-1)
        out = jnp.zeros_like(x)
        num_experts = W1.shape[0]
        for i in range(num_experts):
            mask = (indices == i).astype(x.dtype)[..., None]
            xi = x * mask
            h = jax.nn.relu(xi @ W1[i] + b1[i])
            out = out + (h @ W2[i] + b2[i])
        return out
    x = L0_attn_hidden_states
    x = x + _layernorm(_L0_attn_ref(_layernorm(x, axis=-1), L0_attn_attention_mask, L0_attn_rel_embeddings, L0_attn_Wq, L0_attn_bq, L0_attn_Wk, L0_attn_bk, L0_attn_Wv, L0_attn_bv, L0_attn_Wo, L0_attn_bo, L0_attn_ln_scale, L0_attn_ln_bias), axis=-1)
    x = x + _layernorm(_L0_ffn_ref(_layernorm(x, axis=-1), L0_ffn_W1, L0_ffn_b1, L0_ffn_W2, L0_ffn_b2, L0_ffn_Wr, L0_ffn_br), axis=-1)
    return x

_drawn_inputs = setup_inputs


def setup_inputs(seed=0):
    import zlib

    import numpy as np

    out = dict(_drawn_inputs(seed))
    spreads = {'L0_attn_bq': (0.0, 0.8),
     'L0_attn_bk': (0.0, 0.8),
     'L0_attn_bv': (0.0, 0.1),
     'L0_attn_bo': (0.0, 0.1),
     'L0_attn_ln_scale': (1.0, 0.2),
     'L0_attn_ln_bias': (0.0, 0.1)}
    factors = {'L0_attn_rel_embeddings': 8.0, 'L0_attn_Wq': 8.0, 'L0_attn_Wk': 6.574, 'L0_attn_Wv': 3.19}
    for name, (base, spread) in spreads.items():
        noise = np.random.default_rng([zlib.crc32(name.encode()), seed]).standard_normal(out[name].shape)
        drawn = base * np.exp(spread * noise) if base else spread * noise
        out[name] = jnp.asarray(drawn.astype(out[name].dtype))
    for name, factor in factors.items():
        out[name] = (out[name] * factor).astype(out[name].dtype)
    return out
```

```python
from contextlib import ExitStack

import numpy as np

import concourse.bass as bass
from concourse import mybir
from concourse.alu_op_type import AluOpType as ALU

F32 = mybir.dt.float32
BF16 = mybir.dt.bfloat16
I32 = mybir.dt.int32
U32 = mybir.dt.uint32
ACT = mybir.ActivationFunctionType
AX = mybir.AxisListType

P = 128
B, S, D = 4, 1024, 256
TOK = B * S
NT = TOK // P
H, DH = 16, 16
N = B * H
QT = S // P
SPAN = 64
NBUCKET = 2 * SPAN
MAX_REL = 128
SCALE = float(1.0 / np.sqrt(np.float32(DH * 3)))
E, HID = 8, 1024
ET = NT + E
W3 = 3 * P
BAND = 2 * P - 1
PARTS = 3
QPARTS = (0, 0, 0, 1, 1, 2)
KPARTS = (0, 1, 2, 0, 1, 0)
KROWS = len(QPARTS) * DH
XROWS = KROWS + 9
EPS, EPS_ATT = 1e-5, 1e-7
ROUND = float(1.5 * 2 ** 23)


def buckets():
    rel = np.arange(-(S - 1), S)
    mid = SPAN // 2
    a = np.where((rel < mid) & (rel > -mid), mid - 1, np.abs(rel))
    ratio = np.log((a / mid).astype(np.float32)) / np.float32(np.log(np.float32((MAX_REL - 1) / mid)))
    far = np.ceil(ratio * np.float32(mid - 1)) + mid
    return rel, np.where(a <= mid, a, far * np.sign(rel)).astype(np.int64)


def constants():
    rel, bucket = buckets()
    of = dict(zip(rel.tolist(), bucket.tolist()))
    c2p = lambda r: min(max(of[r] + SPAN, 0), NBUCKET - 1)
    p2c = lambda r: min(max(-of[-r] + SPAN, 0), NBUCKET - 1)
    right, left = NBUCKET - 1, 0
    for r in range(P, S):
        assert (c2p(r), p2c(r), c2p(-r), p2c(-r)) == (right, right, left, left)
    pick = np.zeros((2, NBUCKET, 2 * P), np.float32)
    for v in range(BAND):
        for tab, r, table in ((0, P - 1 - v, c2p), (1, v - (P - 1), p2c)):
            pick[tab, table(r), v] += 1
            pick[tab, right if r >= 0 else left, v] -= 1
    pick[:, left, BAND] += 1
    pick[:, right, BAND] -= 1
    k, m = np.arange(P)[:, None], np.arange(P)[None, :]
    masks = np.zeros((P, 5, P), np.float32)
    masks[:, 0] = m > k
    masks[:, 1] = m < k
    masks[:, 2] = k < m
    masks[:, 3] = 1.0
    masks[:, 4] = k == m
    fold = np.zeros((P, DH), np.float32)
    fold[np.arange(P), np.arange(P) % 32 % DH] = np.arange(P) % 32 < DH
    side = np.zeros((P, 2, 8), np.float32)
    side[np.arange(P), :, np.arange(P) // DH] = 1.0
    steps = np.zeros((P, ET + 8), np.float32)
    steps[:] = np.concatenate([np.arange(ET), np.arange(8)])
    return dict(c_pick=pick, c_masks=masks, c_fold=fold, c_side=side, c_steps=steps)


def build(nc, x, Wq, bq, Wk, bk, Wv, bv, Wo, bo, rel_emb, ln_s, ln_b, W1, b1, W2, b2, Wr, br,
          c_pick, c_masks, c_fold, c_side, c_steps, out):
    ctx = ExitStack()
    with ctx:
        def sem(name):
            return ctx.enter_context(nc.semaphore(name))

        def dram(name, shape, dt=F32):
            return nc.dram_tensor(name, shape, dt)

        xn_d = dram("xn_d", [TOK, D])
        split_d = dram("split_d", [2, PARTS, N * DH, S], BF16)
        far_d = dram("far_d", [2, 2, N, PARTS, S], BF16)
        v_d = dram("v_d", [N, S, DH])
        pick_d = dram("pick_d", [2, PARTS, N * DH, 2 * P], BF16)
        skew_d = dram("skew_d", [2, 2, QT, P * W3 + 2 * P])
        posT_d = dram("posT_d", [P, 2 * 2 * 8])
        ctx_d = dram("ctx_d", [N, S, DH])
        x2_d = dram("x2_d", [TOK, D])
        xf_d = dram("xf_d", [TOK, D])
        xs_d = dram("xs_d", [ET * P, D])
        ys_d = dram("ys_d", [ET * P, D])

        spread(nc, sem, Wk, bk, rel_emb, c_pick, c_masks, c_side, pick_d, skew_d, xs_d, posT_d)
        project(nc, sem, x, Wq, bq, Wk, bk, Wv, bv, c_masks, posT_d, xn_d, split_d, far_d, v_d)
        attend(nc, sem, c_masks, c_fold, split_d, far_d, v_d, pick_d, skew_d, ctx_d)
        sort_d = dram("sort_d", [P, NT], I32)
        expert_d = dram("expert_d", [1, ET], I32)
        total_d = dram("total_d", [1, D])
        mix(nc, sem, x, xn_d, ctx_d, Wo, bo, ln_s, ln_b, Wr, br, c_masks, c_steps, x2_d, xf_d,
            sort_d, expert_d)
        constant_rows(nc, sem, b1, W2, b2, total_d)
        dispatch(nc, sem, xf_d, sort_d, xs_d)
        experts(nc, sem, W1, b1, W2, c_masks, expert_d, total_d, xs_d, ys_d)
        finish(nc, sem, x2_d, sort_d, ys_d, out)



def view(t, offset, dims):
    return bass.AP(tensor=t, offset=offset, ap=dims)


class Stages:

    def __init__(self, semaphore, *names):
        self.sem, self.names = semaphore, names

    def after(self, step, name):
        return step * len(self.names) + (self.names.index(name) + 2)

    def before(self, step):
        return step * len(self.names) + 1


def spread(nc, sem, Wk, bk, rel_emb, c_pick, c_masks, c_side, pick_d, skew_d, xs_d, posT_d):
    with ExitStack() as ctx:
        def sb(name, shape, dt=F32):
            return ctx.enter_context(nc.sbuf_tensor("s_" + name, shape, dt))

        def ps(name, shape):
            return ctx.enter_context(nc.psum_tensor("s_" + name, shape, F32))

        wk = sb("wk", [P, 2, D])
        bk_row = sb("bk_row", [1, D])
        pick = sb("pick", [P, 2, 2 * P])
        masks = sb("masks", [P, 5, P])
        side = sb("side", [P, 2, 8])
        rel = sb("rel", [P, D])
        relT = sb("relT", [P, 2, P])
        pos = sb("pos", [P, D])
        posT = sb("posT", [P, 2, 2])
        far_w = sb("far_w", [P, 2, 2, 8])
        pick32 = sb("pick32", [P, 2, 2, 2 * P])
        rest = sb("rest", [P, 2, 2, 2 * P])
        part = sb("part", [P, PARTS, 2, 2, 2 * P], BF16)
        zeros = sb("zeros", [P, W3 + 2])
        relT_ps, pos_ps, posT_ps, pick_ps = (ps("relT_ps", [P, 2, P]), ps("pos_ps", [P, D]),
                                             ps("posT_ps", [P, 2, P]), ps("pick_ps", [P, 2, 2, 2 * P]))
        loaded, stored = sem("s_loaded"), sem("s_stored")
        pe_made, act_made, dve_made = sem("s_pe_made"), sem("s_act_made"), sem("s_dve_made")
        block = ctx.enter_context(nc.Block())

        @block.sync
        def _(sp):
            loads = [(wk[:, :, :], Wk.rearrange("(k p) n -> p k n", p=P)),
                     (bk_row[:, :], bk.rearrange("(a n) -> a n", a=1)),
                     (pick[:, 0, :], c_pick[0, :, :]), (pick[:, 1, :], c_pick[1, :, :]),
                     (masks[:, :, :], c_masks), (side[:, :, :], c_side), (rel[:, :], rel_emb)]
            assert len(loads) == 7
            for dst, src in loads:
                sp.dma_start(dst, src, allow_slow_non_contiguous=True).then_inc(loaded, 16)
            sp.wait_ge(dve_made, 1)
            for i in range(2):
                for j in range(2):
                    for t in range(QT):
                        sp.dma_start(skew_d[i, j, t, :].rearrange("(p w) -> p w", p=P),
                                     zeros[:, :]).then_inc(stored, 16)
            with sp.Fori(0, ET) as t:
                sp.dma_start(xs_d[bass.ts(t, P), :], zeros[:, 0:D]).then_inc(stored, 16)
            sp.wait_ge(dve_made, 4)
            sp.wait_ge(act_made, 6)
            for b in range(B):
                for tab in range(2):
                    for n in range(PARTS):
                        sp.dma_start(pick_d[tab, n, b * D:(b + 1) * D, :].rearrange("(c p) v -> p c v", p=P),
                                     part[:, n, tab, :, :]).then_inc(stored, 16)
            sp.dma_start(posT_d[:, :], far_w[:, :, :, :].rearrange("p c s h -> p (c s h)")).then_inc(stored, 16)
            sp.wait_ge(stored, 16 * (4 * QT + ET + B * 2 * PARTS + 1))

        @block.tensor
        def _(pe):
            pe.wait_ge(loaded, 16 * 7)
            ident = masks[:, 4, :]
            for c in range(2):
                last = nc.tensor.transpose(relT_ps[:, c, :], rel[:, c * P:(c + 1) * P], ident)
            last.then_inc(pe_made, 1)
            pe.wait_ge(act_made, 1)
            for c in range(2):
                nc.tensor.matmul(pos_ps[:, :], relT[:, c, :], wk[:, c, :], start=(c == 0), stop=False)
            nc.tensor.matmul(pos_ps[:, :], masks[0:1, 3, :], bk_row[:, :], start=False, stop=True).then_inc(pe_made, 1)
            pe.wait_ge(act_made, 2)
            for c in range(2):
                nc.tensor.transpose(posT_ps[:, c, :], pos[:, c * P:(c + 1) * P], ident)
                for tab in range(2):
                    last = nc.tensor.matmul(pick_ps[:, tab, c, :], pos[:, c * P:(c + 1) * P], pick[:, tab, :],
                                            start=True, stop=True)
            last.then_inc(pe_made, 1)

        @block.scalar
        def _(act):
            act.wait_ge(pe_made, 1)
            nc.scalar.copy(relT[:, :, :], relT_ps[:, :, :]).then_inc(act_made, 1)
            act.wait_ge(pe_made, 2)
            nc.scalar.copy(pos[:, :], pos_ps[:, :]).then_inc(act_made, 1)
            act.wait_ge(pe_made, 3)
            nc.scalar.copy(posT[:, :, :], posT_ps[:, :, 0:P:P - 1]).then_inc(act_made, 1)
            for tab in range(2):
                last = nc.scalar.copy(pick32[:, tab, :, :], pick_ps[:, tab, :, :])
            last.then_inc(act_made, 1)
            act.wait_ge(act_made, 4)
            nc.scalar.copy(part[:, 0, :, :, :], pick32[:, :, :, :]).then_inc(act_made, 1)
            act.wait_ge(dve_made, 3)
            nc.scalar.copy(part[:, 1, :, :, :], rest[:, :, :, :]).then_inc(act_made, 1)

        @block.vector
        def _(dve):
            nc.vector.memset(zeros[:, :], 0.0).then_inc(dve_made, 1)
            dve.wait_ge(loaded, 16 * 7)
            dve.wait_ge(act_made, 3)
            for c in range(2):
                for s in range(2):
                    last = nc.vector.tensor_scalar(far_w[:, c, s, :], side[:, 0, :], posT[:, c, s:s + 1], None, ALU.mult)
            last.then_inc(dve_made, 1)
            dve.wait_ge(act_made, 5)
            nc.vector.tensor_tensor(rest[:, :, :, :], pick32[:, :, :, :], part[:, 0, :, :, :], ALU.subtract).then_inc(dve_made, 1)
            dve.wait_ge(act_made, 6)
            nc.vector.tensor_tensor(part[:, 2, :, :, :], rest[:, :, :, :], part[:, 1, :, :, :], ALU.subtract).then_inc(dve_made, 1)


def project(nc, sem, x, Wq, bq, Wk, bk, Wv, bv, c_masks, posT_d, xn_d, split_d, far_d, v_d):
    G = 512
    GT = G // P
    with ExitStack() as ctx:
        def sb(name, shape, dt=F32):
            return ctx.enter_context(nc.sbuf_tensor("p_" + name, shape, dt))

        def ps(name, shape):
            return ctx.enter_context(nc.psum_tensor("p_" + name, shape, F32))

        wq, wk, wv = (sb(n, [P, 2, D]) for n in ("wq", "wk", "wv"))
        bqk = sb("bqk", [P, 4])
        bv_b = sb("bv_b", [P, D])
        masks = sb("masks", [P, 5, P])
        far_w = sb("far_w", [P, 2, 16])
        xt, xn, v32 = (sb(n, [P, GT, D]) for n in ("xt", "xn", "v32"))
        stats = sb("stats", [P, GT, 6])
        mv = sb("mv", [P, GT, 2])
        std, rstd = sb("std", [P, GT]), sb("rstd", [P, GT])
        xT = sb("xT", [P, 2, G])
        qk32, rest = sb("qk32", [P, 4, G]), sb("rest", [P, 4, G])
        part = sb("part", [P, PARTS, 4, G], BF16)
        far32, far_rest = sb("far32", [16, 4, G]), sb("far_rest", [16, 4, G])
        far_part = sb("far_part", [16, PARTS, 4, G], BF16)
        big = ps("big", [P, 4, G])
        tr = ps("tr", [P, 2, G])
        v_ps = ps("v_ps", [P, GT, D])
        held = sem("p_held")
        loaded, xin, stored = sem("p_loaded"), sem("p_xin"), sem("p_stored")
        pe_s = Stages(sem("p_pe"), "turned", "qk", "v", "far")
        act_s = Stages(sem("p_act"), "root", "xT", "hi", "mid", "far32", "far_hi", "far_mid")
        dve_s = Stages(sem("p_dve"), "stats", "moments", "eps", "inverse", "normal", "qk", "v", "rest", "lo",
                       "far_rest", "far_lo")
        STORES = 1 + 2 * 2 * PARTS + 2 * 2 * 2 * PARTS + H

        def hold(eng, semaphore, value):
            eng.wait_ge(semaphore, value)
            eng.sem_inc(held, 1)

        block = ctx.enter_context(nc.Block())

        @block.sync
        def _(sp):
            loads = [(wq[:, :, :], Wq.rearrange("(k p) n -> p k n", p=P)),
                     (wk[:, :, :], Wk.rearrange("(k p) n -> p k n", p=P)),
                     (wv[:, :, :], Wv.rearrange("(k p) n -> p k n", p=P)),
                     (bqk[:, 0:2], bq.rearrange("(c p) -> p c", p=P)),
                     (bqk[:, 2:4], bk.rearrange("(c p) -> p c", p=P)),
                     (bv_b[:, :], view(bv.tensor, 0, [[0, P], [1, D]])),
                     (masks[:, :, :], c_masks), (far_w[:, :, :], posT_d[:, :].rearrange("p (c s) -> p c s", c=2))]
            assert len(loads) == 8
            sp.sem_inc(stored, 16)
            for dst, src in loads:
                sp.dma_start(dst, src, allow_slow_non_contiguous=True).then_inc(loaded, 16)
            with sp.Fori(0, B) as b:
                for g in range(2):
                    step = b * 2 + g
                    row = b * S + g * G
                    hold(sp, dve_s.sem, dve_s.before(step))
                    sp.dma_start(xt[:, :, :], view(x.tensor, row * D, [[D, P], [P * D, GT], [1, D]])).then_inc(xin, 16)
                    hold(sp, dve_s.sem, dve_s.after(step, "normal"))
                    sp.dma_start(view(xn_d, row * D, [[D, P], [P * D, GT], [1, D]]), xn[:, :, :]).then_inc(stored, 16)
                    hold(sp, dve_s.sem, dve_s.after(step, "v"))
                    for h in range(H):
                        sp.dma_start(view(v_d, (b * (H * S) + (h * S + g * G)) * DH, [[DH, P], [P * DH, GT], [1, DH]]),
                                     v32[:, :, h * DH:(h + 1) * DH]).then_inc(stored, 16)
                    hold(sp, dve_s.sem, dve_s.after(step, "lo"))
                    for m in range(4):
                        for n in range(PARTS):
                            at = ((m // 2 * PARTS + n) * (N * DH) + m % 2 * P) * S + g * G
                            sp.dma_start(view(split_d, b * (D * S) + at, [[S, P], [1, G]]), part[:, n, m, :]).then_inc(stored, 16)
                    hold(sp, dve_s.sem, dve_s.after(step, "far_lo"))
                    for m in range(4):
                        for s in range(2):
                            for n in range(PARTS):
                                at = (((m // 2 * 2 + s) * N + m % 2 * 8) * PARTS + n) * S + g * G
                                sp.dma_start(view(far_d, b * (H * PARTS * S) + at, [[PARTS * S, 8], [1, G]]),
                                             far_part[s * 8:(s + 1) * 8, n, m, :]).then_inc(stored, 16)
                    hold(sp, stored, step * (16 * STORES) + 16 * STORES + 16)

        @block.vector
        def _(dve):
            dve.sem_inc(dve_s.sem, 1)
            dve.wait_ge(loaded, 16 * 8)
            with dve.Fori(0, TOK // G) as step:
                s = dve_s
                dve.wait_ge(xin, step * 16 + 16)
                for t in range(GT):
                    last = nc.vector.bn_stats(stats[:, t, :], xt[:, t, :])
                last.then_inc(s.sem, 1)
                dve.wait_ge(s.sem, s.after(step, "stats"))
                dve.sem_inc(held, 1)
                for t in range(GT):
                    last = nc.vector.bn_aggr(mv[:, t, :], stats[:, t, :])
                last.then_inc(s.sem, 1)
                dve.wait_ge(s.sem, s.after(step, "moments"))
                nc.vector.tensor_scalar_add(std[:, :], mv[:, :, 1], EPS).then_inc(s.sem, 1)
                dve.wait_ge(act_s.sem, act_s.after(step, "root"))
                nc.vector.reciprocal(rstd[:, :], std[:, :]).then_inc(s.sem, 1)
                dve.wait_ge(s.sem, s.after(step, "inverse"))
                dve.wait_ge(stored, step * (16 * STORES) + 16)
                for t in range(GT):
                    last = nc.vector.tensor_scalar(xn[:, t, :], xt[:, t, :], mv[:, t, 0:1], rstd[:, t:t + 1],
                                                   ALU.subtract, ALU.mult)
                last.then_inc(s.sem, 1)
                dve.wait_ge(pe_s.sem, pe_s.after(step, "qk"))
                for m in range(4):
                    last = nc.vector.tensor_scalar_add(qk32[:, m, :], big[:, m, :], bqk[:, m:m + 1])
                last.then_inc(s.sem, 1)
                dve.wait_ge(pe_s.sem, pe_s.after(step, "v"))
                nc.vector.tensor_tensor(v32[:, :, :], v_ps[:, :, :],
                                        bv_b[:, :].unsqueeze(1).to_broadcast([P, GT, D]), ALU.add).then_inc(s.sem, 1)
                dve.wait_ge(act_s.sem, act_s.after(step, "hi"))
                nc.vector.tensor_tensor(rest[:, :, :], qk32[:, :, :], part[:, 0, :, :], ALU.subtract).then_inc(s.sem, 1)
                dve.wait_ge(act_s.sem, act_s.after(step, "mid"))
                nc.vector.tensor_tensor(part[:, 2, :, :], rest[:, :, :], part[:, 1, :, :], ALU.subtract).then_inc(s.sem, 1)
                dve.wait_ge(act_s.sem, act_s.after(step, "far_hi"))
                nc.vector.tensor_tensor(far_rest[:, :, :], far32[:, :, :], far_part[:, 0, :, :], ALU.subtract).then_inc(s.sem, 1)
                dve.wait_ge(act_s.sem, act_s.after(step, "far_mid"))
                nc.vector.tensor_tensor(far_part[:, 2, :, :], far_rest[:, :, :], far_part[:, 1, :, :],
                                        ALU.subtract).then_inc(s.sem, 1)

        @block.scalar
        def _(act):
            act.sem_inc(act_s.sem, 1)
            with act.Fori(0, TOK // G) as step:
                s = act_s
                act.wait_ge(dve_s.sem, dve_s.after(step, "eps"))
                nc.scalar.activation(std[:, :], std[:, :], ACT.Sqrt).then_inc(s.sem, 1)
                act.wait_ge(pe_s.sem, pe_s.after(step, "turned"))
                nc.scalar.copy(xT[:, :, :], tr[:, :, :]).then_inc(s.sem, 1)
                act.wait_ge(dve_s.sem, dve_s.after(step, "qk"))
                nc.scalar.copy(part[:, 0, :, :], qk32[:, :, :]).then_inc(s.sem, 1)
                act.wait_ge(dve_s.sem, dve_s.after(step, "rest"))
                nc.scalar.copy(part[:, 1, :, :], rest[:, :, :]).then_inc(s.sem, 1)
                act.wait_ge(pe_s.sem, pe_s.after(step, "far"))
                nc.scalar.copy(far32[:, :, :], big[0:16, :, :]).then_inc(s.sem, 1)
                act.wait_ge(s.sem, s.after(step, "far32"))
                nc.scalar.copy(far_part[:, 0, :, :], far32[:, :, :]).then_inc(s.sem, 1)
                act.wait_ge(dve_s.sem, dve_s.after(step, "far_rest"))
                nc.scalar.copy(far_part[:, 1, :, :], far_rest[:, :, :]).then_inc(s.sem, 1)

        @block.tensor
        def _(pe):
            pe.sem_inc(pe_s.sem, 1)
            pe.wait_ge(loaded, 16 * 8)
            with pe.Fori(0, TOK // G) as step:
                s = pe_s
                pe.wait_ge(dve_s.sem, dve_s.after(step, "normal"))
                for t in range(GT):
                    for k in range(2):
                        last = nc.tensor.transpose(tr[:, k, t * P:(t + 1) * P], xn[:, t, k * P:(k + 1) * P], masks[:, 4, :])
                last.then_inc(s.sem, 1)
                pe.wait_ge(act_s.sem, act_s.after(step, "xT"))
                for m in range(4):
                    w = (wq, wk)[m // 2]
                    for k in range(2):
                        last = nc.tensor.matmul(big[:, m, :], w[:, k, m % 2 * P:(m % 2 + 1) * P], xT[:, k, :],
                                                start=(k == 0), stop=(k == 1))
                last.then_inc(s.sem, 1)
                for t in range(GT):
                    for k in range(2):
                        last = nc.tensor.matmul(v_ps[:, t, :], xT[:, k, t * P:(t + 1) * P], wv[:, k, :],
                                                start=(k == 0), stop=(k == 1))
                last.then_inc(s.sem, 1)
                pe.wait_ge(dve_s.sem, dve_s.after(step, "qk"))
                for m in range(4):
                    last = nc.tensor.matmul(big[0:16, m, :], far_w[:, m % 2, :], qk32[:, m, :], start=True, stop=True)
                last.then_inc(s.sem, 1)

def attend(nc, sem, c_masks, c_fold, split_d, far_d, v_d, pick_d, skew_d, ctx_d):
    SLOT = P * W3 + 2 * P
    HATS = 18
    with ExitStack() as ctx:
        def sb(name, shape, dt=F32):
            return ctx.enter_context(nc.sbuf_tensor("t_" + name, shape, dt))

        masks = sb("masks", [P, 5, P])
        fold = sb("fold", [P, DH])
        ones = sb("ones", [9, S], BF16)
        zeros = sb("zeros", [9, S], BF16)
        keys = [sb(f"keys{i}", [XROWS, S], BF16) for i in range(2)]
        after = [sb(f"after{i}", [XROWS, S], BF16) for i in range(2)]
        before = [sb(f"before{i}", [XROWS, S], BF16) for i in range(2)]
        rows = [sb(f"rows{i}", [KROWS, 2, 2 * P], BF16) for i in range(2)]
        vals = [sb(f"vals{i}", [P, QT, 32]) for i in range(2)]
        table = sb("table", [P, 2, 4, 2, 2 * P])
        side = [sb(f"side{i}", [P, 2, QT]) for i in range(2)]
        near = [sb(f"near{i}", [P, 2, QT, W3]) for i in range(2)]
        bent = sb("bent", [P, 4, P])
        probs = sb("probs", [P, 2, S])
        probsT = sb("probsT", [P, 2, QT, 4 * P])
        most = sb("most", [P, 2, 3])
        scaled = sb("scaled", [P, 2, 3])
        shift = sb("shift", [P, 2])
        total = sb("total", [P, 2, 4])
        inverse = sb("inverse", [P, 2, 4])
        sumT = sb("sumT", [P, 4 * P])
        made = [sb(f"made{i}", [P, QT, DH]) for i in range(2)]
        scores_ps = [ctx.enter_context(nc.psum_tensor(f"t_scores{i}", [P, S], F32)) for i in range(2)]
        table_ps = ctx.enter_context(nc.psum_tensor("t_table_ps", [P, 2, 2 * P], F32))
        turn_ps = [ctx.enter_context(nc.psum_tensor(f"t_turn{i}", [P, 4, P], F32)) for i in range(2)]
        sum_ps = ctx.enter_context(nc.psum_tensor("t_sum_ps", [P, 4 * P], F32))

        held = sem("t_held")
        const_in, set_up, rows_set = sem("t_const_in"), sem("t_set_up"), sem("t_rows_set")
        hats_in, vals_in = sem("t_hats_in"), sem("t_vals_in")
        table_made, table_kept = sem("t_table_made"), sem("t_table_kept")
        side_kept, bend_made, bent_in = sem("t_side_kept"), sem("t_bend_made"), sem("t_bent_in")
        skew_out, skew_in = sem("t_skew_out"), sem("t_skew_in")
        scored, seen, shifted, expd = (sem("t_scored"), sem("t_seen"),
                                               sem("t_shifted"), sem("t_expd"))
        turned = [sem("t_turned0"), sem("t_turned1")]
        kept = [sem("t_kept0"), sem("t_kept1")]
        summed, sum_kept, folded, inverted, ctx_made, ctx_out = (
            sem("t_summed"), sem("t_sum_kept"), sem("t_folded"), sem("t_inverted"), sem("t_ctx_made"),
            sem("t_ctx_out"))

        def hold(eng, semaphore, value):
            eng.wait_ge(semaphore, value)
            eng.sem_inc(held, 1)

        block = ctx.enter_context(nc.Block())

        def units(eng, unit):
            for i in range(2):
                unit(i, i, i == 0, False)
            with eng.Fori(1, N // 2 - 1) as k:
                for i in range(2):
                    unit(k * 2 + i, i, False, False)
            for i in range(2):
                unit(N - 2 + i, i, False, i == 1)

        def window(t):
            lo, hi = max(t - 1, 0), min(t + 2, QT)
            return lo, hi, (lo - t + 1) * P, (hi - t + 1) * P

        @block.sync
        def _(sp):
            def load_unit(n, i, early):
                if not early:
                    hold(sp, scored, n * 8 - 8)
                    hold(sp, table_made, n * 8 - 8)
                kq = [[S, DH], [1, S]]
                part = N * DH * S
                at = n * (DH * S)
                for which, dst, groups in ((1, keys[i], ((0, 3, 0, part), (48, 2, 0, part), (80, 1, 0, part))),
                                           (0, after[i], ((0, 3, 0, 0), (48, 2, 1, 0), (80, 1, 2, 0))),
                                           (0, before[i], ((0, 3, 0, 0), (48, 2, 1, 0), (80, 1, 2, 0)))):
                    for row, many, first_part, step in groups:
                        sp.dma_start(dst[row:row + many * DH, :],
                                     view(split_d, at + (which * PARTS + first_part) * part, [[step, many]] + kq)
                                     ).then_inc(hats_in, 16)
                far = N * PARTS * S
                sp.dma_start(keys[i][KROWS:KROWS + 6, :],
                             view(far_d, n * (PARTS * S) + 2 * far, [[far, 2], [S, PARTS], [1, S]])).then_inc(hats_in, 16)
                sp.dma_start(after[i][KROWS + 6:XROWS, :],
                             view(far_d, n * (PARTS * S) + far, [[S, PARTS], [1, S]])).then_inc(hats_in, 16)
                sp.dma_start(before[i][KROWS + 6:XROWS, :],
                             view(far_d, n * (PARTS * S), [[S, PARTS], [1, S]])).then_inc(hats_in, 16)
                wide = 2 * P
                part = N * DH * wide
                for tab, groups in ((0, ((0, 3, 0, part), (48, 2, 0, part), (80, 1, 0, part))),
                                    (1, ((0, 3, 0, 0), (48, 2, 1, 0), (80, 1, 2, 0)))):
                    for row, many, first_part, step in groups:
                        sp.dma_start(rows[i][row:row + many * DH, tab, :],
                                     view(pick_d, n * (DH * wide) + (tab * PARTS + first_part) * part,
                                          [[step, many], [wide, DH], [1, wide]])).then_inc(hats_in, 16)

            def load_vals(n, i, early):
                if not early:
                    hold(sp, summed, n * 2 - 2)
                sp.dma_start(vals[i][:, :, 0:DH], view(v_d, n * (S * DH), [[DH, P], [P * DH, QT], [1, DH]])
                             ).then_inc(vals_in, 16)

            def skew(n, i, early):
                for h in range(2):
                    hold(sp, table_kept, n * 8 + (4 * h + 4))
                    if not early:
                        hold(sp, skew_in, (n * 2 + (h - 3)) * 32)
                    for tab in range(2):
                        at = ((i * 2 + tab) * QT + 4 * h) * SLOT
                        sp.dma_start(view(skew_d, at + 1, [[W3, P], [SLOT, 4], [1, BAND]]),
                                     table[:, h, :, tab, 0:BAND]).then_inc(skew_out, 16)
                    if not early:
                        hold(sp, scored, n * 8 - 8)
                        hold(sp, shifted, n * 8 - 8)
                    hold(sp, skew_out, (n * 2 + (h + 1)) * 32)
                    for tab in range(2):
                        at = ((i * 2 + tab) * QT + 4 * h) * SLOT
                        sp.dma_start(near[i][:, tab, 4 * h:4 * h + 4, :],
                                     view(skew_d, at, [[W3 - 1, P], [SLOT, 4], [1, W3]])).then_inc(skew_in, 16)

            def store(n, i):
                hold(sp, ctx_made, n * 2 + 2)
                sp.dma_start(view(ctx_d, n * (S * DH), [[DH, P], [P * DH, QT], [1, DH]]),
                             made[i][:, :, :]).then_inc(ctx_out, 16)

            sp.dma_start(masks[:, :, :], c_masks).then_inc(const_in, 16)
            sp.dma_start(fold[:, :], c_fold).then_inc(const_in, 16)
            hold(sp, set_up, 2)
            for i in range(2):
                sp.dma_start(keys[i][KROWS + 6:XROWS, :], ones[0:3, :]).then_inc(rows_set, 16)
                sp.dma_start(after[i][KROWS:KROWS + 3, :], zeros[0:3, :]).then_inc(rows_set, 16)
                sp.dma_start(after[i][KROWS + 3:KROWS + 6, :], ones[0:3, :]).then_inc(rows_set, 16)
                sp.dma_start(before[i][KROWS:KROWS + 3, :], ones[0:3, :]).then_inc(rows_set, 16)
                sp.dma_start(before[i][KROWS + 3:KROWS + 6, :], zeros[0:3, :]).then_inc(rows_set, 16)
            load_unit(0, 0, True)
            load_vals(0, 0, True)
            skew(0, 0, True)

            def unit(n, i, first, last):
                if not last:
                    early = first
                    load_unit(n + 1, 1 - i, early)
                    load_vals(n + 1, 1 - i, early)
                if not first:
                    store(n - 1, 1 - i)
                if not last:
                    skew(n + 1, 1 - i, early)
            units(sp, unit)
            store(N - 1, 1)
            hold(sp, ctx_out, N * 16)

        @block.tensor
        def _(pe):
            ident = masks[:, 4, :]

            def make_table(n, i, u, early):
                if u == 0:
                    pe.wait_ge(hats_in, n * (HATS * 16) + HATS * 16)
                if not (early and u == 0):
                    pe.wait_ge(table_kept, n * 8 + u)
                nc.tensor.matmul(table_ps[:, 0, :], after[i][0:KROWS, u * P:(u + 1) * P], rows[i][:, 0, :],
                                 start=True, stop=False)
                nc.tensor.matmul(table_ps[:, 1, :], keys[i][0:KROWS, u * P:(u + 1) * P], rows[i][:, 1, :],
                                 start=False, stop=True).then_inc(table_made, 1)

            def score(n, i, t, first):
                if not (first and t < 2):
                    pe.wait_ge(expd, n * 8 + (t - 1))
                ps = scores_ps[t % 2]
                lo, hi, _, _ = window(t)
                edge = (t + 1) * P
                cuts = sorted({0, 512, S, edge})
                for a, z in zip(cuts[:-1], cuts[1:]):
                    q = after[i] if z <= edge else before[i]
                    more = any(j * P // 512 == a // 512 for j in range(lo, hi))
                    nc.tensor.matmul(ps[:, a:z], q[:, t * P:(t + 1) * P], keys[i][:, a:z],
                                     start=a % 512 == 0, stop=z % 512 == 0 and not more)
                pe.wait_ge(bent_in, n * 2 + (1 if t < 3 else 2))
                for j in range(lo, hi):
                    final = nc.tensor.matmul(ps[:, j * P:(j + 1) * P],
                                             near[i][:, 1, j, (t - j + 1) * P:(t - j + 2) * P], ident,
                                             start=False, stop=(j == hi - 1 or (j + 1) * P == 512), is_transpose=True)
                final.then_inc(scored, 1)

            def turn(n, t, first):
                pe.wait_ge(expd, n * 8 + (t + 1))
                for h in range(2):
                    if not (first and t == 0):
                        pe.wait_ge(kept[h], n * 8 + t)
                    for j in range(4):
                        final = nc.tensor.transpose(turn_ps[h][:, j, :], probs[:, t % 2, (4 * h + j) * P:(4 * h + j + 1) * P], ident)
                    final.then_inc(turned[h], 1)

            def weigh(n, i, half, first):
                if half == 0:
                    pe.wait_ge(vals_in, n * 16 + 16)
                for h in range(2):
                    pe.wait_ge(kept[h], n * 8 + (4 * half + 4))
                if not (first and half == 0):
                    pe.wait_ge(ctx_made, n * 2 + half)
                for j in range(QT):
                    g = j % 4 * 32
                    final = nc.tensor.matmul(sum_ps[g:g + 32, :], vals[i][:, j, :], probsT[:, half, j, :],
                                             start=(j < 4), stop=(j >= 4), skip_group_check=True)
                final.then_inc(summed, 1)

            def add_groups(n, half):
                pe.wait_ge(sum_kept, n * 2 + (half + 1))
                for q in range(4):
                    final = nc.tensor.matmul(sum_ps[:, q * DH:(q + 1) * DH], sumT[:, q * P:(q + 1) * P], fold[:, :],
                                             start=True, stop=True)
                final.then_inc(folded, 1)

            pe.wait_ge(const_in, 32)
            pe.wait_ge(rows_set, 16 * 10)
            pe.wait_ge(set_up, 4)
            for u in range(QT):
                make_table(0, 0, u, True)

            def unit(n, i, first, last):
                for t in range(QT):
                    tables = not last and 2 <= t < 6
                    if tables:
                        make_table(n + 1, 1 - i, 2 * (t - 2), False)
                    score(n, i, t, first)
                    if t > 0:
                        turn(n, t - 1, first)
                    elif not first:
                        turn(n - 1, QT - 1, False)
                    if tables:
                        make_table(n + 1, 1 - i, 2 * (t - 2) + 1, False)
                    if t == 1 and not first:
                        weigh(n - 1, 1 - i, 1, False)
                    if t == 2 and not first:
                        add_groups(n - 1, 1)
                    if t == 5:
                        weigh(n, i, 0, first)
                    if t == 6:
                        add_groups(n, 0)
            units(pe, unit)
            turn(N - 1, QT - 1, False)
            weigh(N - 1, 1, 1, False)
            add_groups(N - 1, 1)

        @block.vector
        def _(dve):
            def row_max(n, i, t, first):
                ps = scores_ps[t % 2]
                lo, hi, a, z = window(t)
                dve.wait_ge(bent_in, n * 2 + (1 if t < 4 else 2))
                dve.wait_ge(scored, n * 8 + (t + 1))
                many = 1
                for u, v in ((0, lo * P), (hi * P, S)):
                    if v > u:
                        nc.vector.tensor_reduce(most[:, t % 2, many:many + 1], ps[:, u:v], AX.X, ALU.max)
                        many += 1
                nc.vector.tensor_tensor_reduce(ps[:, lo * P:hi * P], ps[:, lo * P:hi * P], near[i][:, 0, t, a:z],
                                               1.0, -3.0e38, ALU.add, ALU.max, accum_out=most[:, t % 2, 0:1]
                                               ).then_inc(seen, 1)
                dve.wait_ge(seen, n * 8 + (t + 1))
                nc.vector.tensor_scalar(scaled[:, t % 2, 0:many], most[:, t % 2, 0:many], -SCALE, None, ALU.mult, ALU.min,
                                        accum_out=shift[:, t % 2:t % 2 + 1]).then_inc(shifted, 1)

            def keep(n, t, first):
                dve.wait_ge(turned[0], n * 8 + (t + 1))
                if not (first and t < 4):
                    dve.wait_ge(summed, n * 2 + (t // 4 - 1))
                nc.vector.tensor_copy(probsT[:, t // 4, 0:4, t % 4 * P:(t % 4 + 1) * P],
                                      turn_ps[0][:, :, :]).then_inc(kept[0], 1)

            def divide(n, i, half, early):
                nc.vector.reciprocal(inverse[:, half, :], total[:, half, :]).then_inc(inverted, 1)
                dve.wait_ge(inverted, n * 2 + (half + 1))
                dve.wait_ge(folded, n * 2 + (half + 1))
                if not early:
                    dve.wait_ge(ctx_out, n * 16 - 16)
                nc.vector.tensor_tensor(made[i][:, 4 * half:4 * half + 4, :],
                                        sum_ps[:, 0:4 * DH].rearrange("p (q d) -> p q d", q=4),
                                        inverse[:, half, :].unsqueeze(2).to_broadcast([P, 4, DH]),
                                        ALU.mult).then_inc(ctx_made, 1)

            nc.vector.memset(ones[:, :], 1.0).then_inc(set_up, 1)
            nc.vector.memset(zeros[:, :], 0.0).then_inc(set_up, 1)
            for i in range(2):
                nc.vector.memset(vals[i][:, :, DH:32], 0.0).then_inc(set_up, 1)

            def unit(n, i, first, last):
                for t in range(QT):
                    row_max(n, i, t, first)
                    if t > 0:
                        keep(n, t - 1, first)
                    elif not first:
                        keep(n - 1, QT - 1, False)
                    if t == 2 and not first:
                        divide(n - 1, 1 - i, 1, isinstance(n, int) and n < 3)
                    if t == 6:
                        divide(n, i, 0, isinstance(n, int) and n < 2)
            units(dve, unit)
            keep(N - 1, QT - 1, False)
            divide(N - 1, 1, 1, False)

        @block.scalar
        def _(act):
            def keep_table(n, i, u, early):
                act.wait_ge(table_made, n * 8 + (u + 1))
                if u % 4 == 0 and not early:
                    h = u // 4
                    act.wait_ge(skew_out, (n * 2 + (h - 1)) * 32)
                    act.wait_ge(side_kept, n * 2 + (h - 1))
                nc.scalar.copy(table[:, u // 4, u % 4, :, :], table_ps[:, :, :]).then_inc(table_kept, 1)

            def exponent(n, t, first):
                act.wait_ge(shifted, n * 8 + (t + 1))
                if not (first and t < 2):
                    act.wait_ge(turned[1], n * 8 + (t - 1))
                if t % 4 == 0 and not (first and t < 4):
                    act.wait_ge(ctx_made, n * 2 + (t // 4 - 1))
                nc.scalar.activation(probs[:, t % 2, :], scores_ps[t % 2][:, :], ACT.Exp, bias=shift[:, t % 2:t % 2 + 1],
                                     scale=SCALE, accum_out=total[:, t // 4, t % 4:t % 4 + 1]).then_inc(expd, 1)

            def keep(n, t, first):
                act.wait_ge(turned[1], n * 8 + (t + 1))
                if not (first and t < 4):
                    act.wait_ge(summed, n * 2 + (t // 4 - 1))
                nc.scalar.copy(probsT[:, t // 4, 4:8, t % 4 * P:(t % 4 + 1) * P], turn_ps[1][:, :, :]).then_inc(kept[1], 1)

            def keep_sum(n, half, first):
                act.wait_ge(summed, n * 2 + (half + 1))
                if not (first and half == 0):
                    act.wait_ge(folded, n * 2 + half)
                nc.scalar.copy(sumT[:, :], sum_ps[:, :]).then_inc(sum_kept, 1)

            for u in range(QT):
                keep_table(0, 0, u, True)

            def unit(n, i, first, last):
                for t in range(QT):
                    tables = not last and 2 <= t < 6
                    if tables:
                        keep_table(n + 1, 1 - i, 2 * (t - 2), False)
                    if t > 0:
                        keep(n, t - 1, first)
                    elif not first:
                        keep(n - 1, QT - 1, False)
                    if tables:
                        keep_table(n + 1, 1 - i, 2 * (t - 2) + 1, False)
                    exponent(n, t, first)
                    if t == 1 and not first:
                        keep_sum(n - 1, 1, False)
                    if t == 5:
                        keep_sum(n, 0, first)
            units(act, unit)
            keep(N - 1, QT - 1, False)
            keep_sum(N - 1, 1, False)

        @block.gpsimd
        def _(pool):
            def bend(n, i):
                for h in range(2):
                    pool.wait_ge(table_kept, n * 8 + (4 * h + 4))
                    column = table[:, h, :, :, BAND]
                    nc.gpsimd.tensor_tensor(side[i][:, :, 4 * h:4 * h + 4].rearrange("p a t -> p t a"),
                                            column, masks[:, 3, 0:8].rearrange("p (t a) -> p t a", a=2),
                                            ALU.mult).then_inc(side_kept, 1)
                    pool.wait_ge(side_kept, n * 2 + (h + 1))
                    pool.wait_ge(skew_in, (n * 2 + (h + 1)) * 32)
                    pool.wait_ge(bent_in, n * 2 + h)
                    for tab in range(2):
                        nc.gpsimd.tensor_tensor(bent[:, :, :], masks[:, tab, :].unsqueeze(1).to_broadcast([P, 4, P]),
                                                side[i][:, tab, 4 * h:4 * h + 4].unsqueeze(2).to_broadcast([P, 4, P]),
                                                ALU.mult).then_inc(bend_made, 1)
                        pool.wait_ge(bend_made, n * 6 + (3 * h + 2 * tab + 1))
                        diag = near[i][:, tab, 4 * h:4 * h + 4, P:2 * P]
                        nc.gpsimd.tensor_tensor(diag, diag, bent[:, :, :], ALU.add
                                                ).then_inc((bend_made, bent_in)[tab], 1)
                        if tab == 0:
                            pool.wait_ge(bend_made, n * 6 + (3 * h + 2))

            pool.wait_ge(const_in, 32)
            bend(0, 0)

            def unit(n, i, first, last):
                if not last:
                    bend(n + 1, 1 - i)
            units(pool, unit)


def mix(nc, sem, x, xn_d, ctx_d, Wo, bo, ln_s, ln_b, Wr, br, c_masks, c_steps, x2_d, xf_d, sort_d, expert_d):
    with ExitStack() as ctx:
        def sb(name, shape, dt=F32):
            return ctx.enter_context(nc.sbuf_tensor("m_" + name, shape, dt))

        def ps(name, shape):
            return ctx.enter_context(nc.psum_tensor("m_" + name, shape, F32))

        wo, wr = sb("wo", [P, 2, D]), sb("wr", [P, 2, E])
        bo_b, ls_b, lb_b, br_b = sb("bo_b", [P, D]), sb("ls_b", [P, D]), sb("lb_b", [P, D]), sb("br_b", [P, E])
        masks, steps = sb("masks", [P, 5, P]), sb("steps", [P, ET + 8])
        ctx_in, xt, xn = sb("ctx_in", [P, H, DH]), sb("xt", [P, D]), sb("xn", [P, D])
        turned, xfT = sb("turned", [P, 2, P]), sb("xfT", [P, 2, P])
        y0, y1, y2, y3, y4, y5, y6, x2, xf = (sb(f"y{i}", [P, D]) for i in range(9))
        logits, top, index = sb("logits", [P, E]), sb("top", [P, E]), sb("index", [P, E], U32)
        choice = sb("choice", [P, NT])
        turn_ps, out_ps, logit_ps = ps("turn_ps", [P, 4, P]), ps("out_ps", [P, 512]), ps("logit_ps", [P, 512])
        before_ps, count_ps = ps("before_ps", [P, 512]), ps("count_ps", [P, 512])
        held = sem("m_held")
        loaded, tile_in, stored = sem("m_loaded"), sem("m_tile_in"), sem("m_stored")
        norms = [[sb(f"{w}{i}", [P, n]) for w, n in (("stats", 6), ("mv", 2), ("var", 1), ("root", 1), ("inv", 1))]
                 for i in range(3)]
        norm_stages = [f"{w}{i}" for i in range(3) for w in ("stats", "mv", "var", "inv", "out")]
        dve_s = Stages(sem("m_dve"), "residual", "bias", *norm_stages[:5], "scaled", "shifted", *norm_stages[5:10],
                       "x2", *norm_stages[10:], "logits", "top", "index", "choice")
        act_s = Stages(sem("m_act"), "turned", "root0", "root1", "root2", "xfT")
        pe_s = Stages(sem("m_pe"), "turned", "out", "xfT", "logits")
        SORTED = 21
        sorting = sem("m_sorting")
        sorted_pe = sem("m_sorted_pe")

        def hold(eng, semaphore, value):
            eng.wait_ge(semaphore, value)
            eng.sem_inc(held, 1)

        block = ctx.enter_context(nc.Block())

        hot = sb("hot", [P, NT, E])
        scan = [sb(f"scan{i}", [P, NT, E]) for i in range(2)]
        counts, base = sb("counts", [P, NT, E]), sb("base", [P, E])
        tiles = sb("tiles", [P, E])
        ends = [sb(f"ends{i}", [P, E]) for i in range(2)]
        places, chosen = sb("places", [P, NT, E]), sb("chosen", [P, NT, E])
        place, place_i = sb("place", [P, NT]), sb("place_i", [P, NT], I32)
        behind, expert, expert_c, expert_i = (sb("behind", [P, ET, E]), sb("expert", [P, ET]), sb("expert_c", [P, ET]),
                                              sb("expert_i", [P, ET], I32))

        @block.sync
        def _(sp):
            def row(src, n):
                return view(src.tensor, 0, [[0, P], [1, n]])
            loads = [(wo[:, :, :], Wo.rearrange("(k p) n -> p k n", p=P)),
                     (wr[:, :, :], Wr.rearrange("(k p) n -> p k n", p=P)),
                     (bo_b[:, :], row(bo, D)), (ls_b[:, :], row(ln_s, D)), (lb_b[:, :], row(ln_b, D)),
                     (br_b[:, :], row(br, E)), (masks[:, :, :], c_masks), (steps[:, :], c_steps)]
            assert len(loads) == 8
            sp.sem_inc(stored, 16)
            for dst, src in loads:
                sp.dma_start(dst, src, allow_slow_non_contiguous=True).then_inc(loaded, 16)
            with sp.Fori(0, B) as b:
                for q in range(QT):
                    step = b * QT + q
                    row0 = b * S + q * P
                    hold(sp, dve_s.sem, dve_s.before(step))
                    sp.dma_start(ctx_in[:, :, :], view(ctx_d, b * (H * S * DH) + q * P * DH,
                                                       [[DH, P], [S * DH, H], [1, DH]])).then_inc(tile_in, 16)
                    sp.dma_start(xt[:, :], view(x.tensor, row0 * D, [[D, P], [1, D]])).then_inc(tile_in, 16)
                    sp.dma_start(xn[:, :], view(xn_d, row0 * D, [[D, P], [1, D]])).then_inc(tile_in, 16)
                    hold(sp, dve_s.sem, dve_s.after(step, "out2"))
                    sp.dma_start(view(x2_d, row0 * D, [[D, P], [1, D]]), x2[:, :]).then_inc(stored, 16)
                    sp.dma_start(view(xf_d, row0 * D, [[D, P], [1, D]]), xf[:, :]).then_inc(stored, 16)
            hold(sp, sorting, SORTED)
            sp.dma_start(sort_d[:, :], place_i[:, :]).then_inc(stored, 16)
            sp.dma_start(expert_d[:, :], expert_i[0:1, :]).then_inc(stored, 16)
            hold(sp, stored, 16 * (2 * NT + 3))

        @block.vector
        def _(dve):
            dve.sem_inc(dve_s.sem, 1)
            s = dve_s
            dve.wait_ge(loaded, 16 * 8)
            with dve.Fori(0, NT) as step:
                def own(name):
                    dve.wait_ge(s.sem, s.after(step, name))

                def norm(i, src, dst, eps):
                    stats, mv, var, root, inv = norms[i]
                    nc.vector.bn_stats(stats[:, :], src[:, :]).then_inc(s.sem, 1)
                    own(f"stats{i}")
                    dve.sem_inc(held, 1)
                    nc.vector.bn_aggr(mv[:, :], stats[:, :]).then_inc(s.sem, 1)
                    own(f"mv{i}")
                    nc.vector.tensor_scalar_add(var[:, :], mv[:, 1:2], eps).then_inc(s.sem, 1)
                    dve.wait_ge(act_s.sem, act_s.after(step, f"root{i}"))
                    nc.vector.reciprocal(inv[:, :], root[:, :]).then_inc(s.sem, 1)
                    own(f"inv{i}")
                    nc.vector.tensor_scalar(dst[:, :], src[:, :], mv[:, 0:1], inv[:, :], ALU.subtract, ALU.mult
                                            ).then_inc(s.sem, 1)
                    own(f"out{i}")

                dve.wait_ge(tile_in, step * 48 + 48)
                dve.wait_ge(pe_s.sem, pe_s.after(step, "out"))
                nc.vector.tensor_tensor(y0[:, :], out_ps[:, 0:D], xn[:, :], ALU.add).then_inc(s.sem, 1)
                own("residual")
                nc.vector.tensor_tensor(y1[:, :], y0[:, :], bo_b[:, :], ALU.add).then_inc(s.sem, 1)
                own("bias")
                norm(0, y1, y2, EPS_ATT)
                nc.vector.tensor_tensor(y3[:, :], y2[:, :], ls_b[:, :], ALU.mult).then_inc(s.sem, 1)
                own("scaled")
                nc.vector.tensor_tensor(y4[:, :], y3[:, :], lb_b[:, :], ALU.add).then_inc(s.sem, 1)
                own("shifted")
                norm(1, y4, y5, EPS)
                dve.wait_ge(stored, step * 32 + 16)
                nc.vector.tensor_tensor(x2[:, :], xt[:, :], y5[:, :], ALU.add).then_inc(s.sem, 1)
                own("x2")
                norm(2, x2, xf, EPS)
                dve.wait_ge(pe_s.sem, pe_s.after(step, "logits"))
                nc.vector.tensor_tensor(logits[:, :], logit_ps[:, 0:E], br_b[:, :], ALU.add).then_inc(s.sem, 1)
                own("logits")
                dve.sem_inc(held, 1)
                nc.vector.max(top[:, :], logits[:, :]).then_inc(s.sem, 1)
                own("top")
                dve.sem_inc(held, 1)
                nc.vector.max_index(index[:, :], top[:, :], logits[:, :]).then_inc(s.sem, 1)
                own("index")
                nc.vector.tensor_copy(choice[:, bass.ts(step, 1)], index[:, 0:1]).then_inc(s.sem, 1)
            count = [0]

            def link(instruction):
                instruction.then_inc(sorting, 1)
                count[0] += 1
                dve.wait_ge(sorting, count[0])

            dve.wait_ge(s.sem, s.before(NT))
            link(nc.vector.tensor_tensor(hot[:, :, :], choice[:, :].unsqueeze(2).to_broadcast([P, NT, E]),
                                         steps[:, ET:ET + E].unsqueeze(1).to_broadcast([P, NT, E]), ALU.is_equal))
            dve.wait_ge(sorted_pe, 1)
            link(nc.vector.tensor_copy(counts[:, :, :], count_ps[:, 0:NT * E].rearrange("p (t e) -> p t e", e=E)))
            src, k = counts, 0
            d = 1
            while d < NT:
                dst = scan[k % 2]
                nc.vector.tensor_copy(dst[:, 0:d, :], src[:, 0:d, :])
                link(nc.vector.tensor_tensor(dst[:, d:NT, :], src[:, d:NT, :], src[:, 0:NT - d, :], ALU.add))
                src, k, d = dst, k + 1, 2 * d
            upto = src
            link(nc.vector.tensor_scalar(tiles[:, :], upto[:, NT - 1, :], 1.0 / P, 0.5 - 1.0 / (2 * P), ALU.mult, ALU.add))
            link(nc.vector.tensor_scalar(base[:, :], tiles[:, :], ROUND, -ROUND, ALU.add, ALU.add))
            link(nc.vector.tensor_copy(tiles[:, :], base[:, :]))
            src, k, d = tiles, 0, 1
            while d < E:
                dst = ends[k % 2]
                nc.vector.tensor_copy(dst[:, 0:d], src[:, 0:d])
                link(nc.vector.tensor_tensor(dst[:, d:E], src[:, d:E], src[:, 0:E - d], ALU.add))
                src, k, d = dst, k + 1, 2 * d
            end = src
            nc.vector.tensor_tensor(behind[:, :, :], steps[:, 0:ET].unsqueeze(2).to_broadcast([P, ET, E]),
                                    end[:, :].unsqueeze(1).to_broadcast([P, ET, E]), ALU.is_ge)
            link(nc.vector.tensor_tensor(base[:, :], end[:, :], tiles[:, :], ALU.subtract))
            nc.vector.tensor_reduce(expert[:, :], behind[:, :, :], AX.X, ALU.add)
            link(nc.vector.tensor_tensor(places[:, :, :], upto[:, :, :], counts[:, :, :], ALU.subtract))
            link(nc.vector.tensor_tensor(chosen[:, :, :], places[:, :, :],
                                         before_ps[:, 0:NT * E].rearrange("p (t e) -> p t e", e=E), ALU.add))
            link(nc.vector.tensor_scalar(tiles[:, :], base[:, :], float(P), None, ALU.mult))
            nc.vector.tensor_scalar_min(expert_c[:, :], expert[:, :], float(E - 1))
            link(nc.vector.tensor_tensor(places[:, :, :], chosen[:, :, :],
                                         tiles[:, :].unsqueeze(1).to_broadcast([P, NT, E]), ALU.add))
            nc.vector.tensor_copy(expert_i[:, :], expert_c[:, :])
            link(nc.vector.tensor_tensor(chosen[:, :, :], places[:, :, :], hot[:, :, :], ALU.mult))
            link(nc.vector.tensor_reduce(place[:, :], chosen[:, :, :], AX.X, ALU.add))
            link(nc.vector.tensor_copy(place_i[:, :], place[:, :]))
            assert count[0] == SORTED, count[0]

        @block.scalar
        def _(act):
            act.sem_inc(act_s.sem, 1)
            with act.Fori(0, NT) as step:
                act.wait_ge(pe_s.sem, pe_s.after(step, "turned"))
                nc.scalar.copy(turned[:, :, :], turn_ps[:, 0:2, :]).then_inc(act_s.sem, 1)
                for i in range(3):
                    act.wait_ge(dve_s.sem, dve_s.after(step, f"var{i}"))
                    nc.scalar.activation(norms[i][3][:, :], norms[i][2][:, :], ACT.Sqrt).then_inc(act_s.sem, 1)
                act.wait_ge(pe_s.sem, pe_s.after(step, "xfT"))
                nc.scalar.copy(xfT[:, :, :], turn_ps[:, 2:4, :]).then_inc(act_s.sem, 1)

        @block.tensor
        def _(pe):
            pe.sem_inc(pe_s.sem, 1)
            pe.wait_ge(loaded, 16 * 8)
            ident = masks[:, 4, :]
            with pe.Fori(0, NT) as step:
                pe.wait_ge(tile_in, step * 48 + 48)
                pe.wait_ge(act_s.sem, act_s.before(step))
                for k in range(2):
                    last = nc.tensor.transpose(turn_ps[:, k, :], ctx_in[:, :, :].rearrange("p h d -> p (h d)")[:, k * P:(k + 1) * P], ident)
                last.then_inc(pe_s.sem, 1)
                pe.wait_ge(act_s.sem, act_s.after(step, "turned"))
                for k in range(2):
                    last = nc.tensor.matmul(out_ps[:, 0:D], turned[:, k, :], wo[:, k, :], start=(k == 0), stop=(k == 1))
                last.then_inc(pe_s.sem, 1)
                pe.wait_ge(dve_s.sem, dve_s.after(step, "out2"))
                for k in range(2):
                    last = nc.tensor.transpose(turn_ps[:, 2 + k, :], xf[:, k * P:(k + 1) * P], ident)
                last.then_inc(pe_s.sem, 1)
                pe.wait_ge(act_s.sem, act_s.after(step, "xfT"))
                for k in range(2):
                    last = nc.tensor.matmul(logit_ps[:, 0:E], xfT[:, k, :], wr[:, k, :], start=(k == 0), stop=(k == 1))
                last.then_inc(pe_s.sem, 1)
            pe.wait_ge(sorting, 1)
            hot2 = hot[:, :, :].rearrange("p t e -> p (t e)")
            nc.tensor.matmul(before_ps[:, 0:NT * E], masks[:, 2, :], hot2, start=True, stop=True)
            nc.tensor.matmul(count_ps[:, 0:NT * E], masks[:, 3, :], hot2, start=True, stop=True).then_inc(sorted_pe, 1)


def constant_rows(nc, sem, b1, W2, b2, total_d):
    KC = HID // P
    with ExitStack() as ctx:
        w2 = [ctx.enter_context(nc.sbuf_tensor(f"c_w2_{i}", [P, KC, D], F32)) for i in range(2)]
        b1_sb = ctx.enter_context(nc.sbuf_tensor("c_b1", [P, E, KC], F32))
        r1 = ctx.enter_context(nc.sbuf_tensor("c_r1", [P, E, KC], F32))
        b2_sb = ctx.enter_context(nc.sbuf_tensor("c_b2", [E, D], F32))
        ones = ctx.enter_context(nc.sbuf_tensor("c_ones", [E, 1], F32))
        row = ctx.enter_context(nc.sbuf_tensor("c_row", [1, D], F32))
        row_ps = ctx.enter_context(nc.psum_tensor("c_row_ps", [1, 512], F32))
        loaded, made, used, stored = sem("c_loaded"), sem("c_made"), sem("c_used"), sem("c_stored")
        w2_in = [sem("c_w2_in0"), sem("c_w2_in1")]
        block = ctx.enter_context(nc.Block())

        @block.sync
        def _(sp):
            sp.dma_start(b1_sb[:, :, :], b1.rearrange("e (c p) -> p e c", p=P),
                         allow_slow_non_contiguous=True).then_inc(loaded, 16)
            sp.dma_start(b2_sb[:, :], b2).then_inc(loaded, 16)
            for e in range(E):
                if e >= 2:
                    sp.wait_ge(used, e - 1)
                sp.dma_start(w2[e % 2][:, :, :], W2[e, :, :].rearrange("(c p) n -> p c n", p=P)).then_inc(w2_in[e % 2], 16)
            sp.wait_ge(made, 3)
            sp.dma_start(total_d[:, :], row[:, :]).then_inc(stored, 16)
            sp.wait_ge(stored, 16)

        @block.vector
        def _(dve):
            nc.vector.memset(ones[:, :], 1.0).then_inc(made, 1)
            dve.wait_ge(loaded, 32)
            nc.vector.tensor_scalar_max(r1[:, :, :], b1_sb[:, :, :], 0.0).then_inc(made, 1)
            dve.wait_ge(used, E + 1)
            nc.vector.tensor_copy(row[:, :], row_ps[:, 0:D]).then_inc(made, 1)

        @block.tensor
        def _(pe):
            pe.wait_ge(made, 2)
            for e in range(E):
                pe.wait_ge(w2_in[e % 2], 16 * (e // 2 + 1))
                for c in range(KC):
                    last = nc.tensor.matmul(row_ps[:, 0:D], r1[:, e, c:c + 1], w2[e % 2][:, c, :],
                                            start=(e == 0 and c == 0), stop=False)
                last.then_inc(used, 1)
            nc.tensor.matmul(row_ps[:, 0:D], ones[:, :], b2_sb[:, :], start=False, stop=True).then_inc(used, 1)


def dispatch(nc, sem, xf_d, sort_d, xs_d):
    with ExitStack() as ctx:
        place = ctx.enter_context(nc.sbuf_tensor("d_place", [P, NT], I32))
        rows = [ctx.enter_context(nc.sbuf_tensor(f"d_rows{i}", [P, D], F32)) for i in range(4)]
        loaded = sem("d_loaded")
        row_in, sent = ([sem(f"d_{w}{i}") for i in range(4)] for w in ("row_in", "sent"))
        block = ctx.enter_context(nc.Block())

        @block.sync
        def _(sp):
            sp.dma_start(place[:, :], sort_d[:, :]).then_inc(loaded, 16)
            for t in range(NT):
                if t >= 4:
                    sp.wait_ge(sent[t % 4], 16 * (t // 4))
                sp.dma_start(rows[t % 4][:, :], xf_d[t * P:(t + 1) * P, :]).then_inc(row_in[t % 4], 16)

        @block.gpsimd
        def _(pool):
            pool.wait_ge(loaded, 16)
            for t in range(NT):
                pool.wait_ge(row_in[t % 4], 16 * (t // 4 + 1))
                nc.gpsimd.indirect_dma_start(xs_d[:, :], bass.IndirectOffsetOnAxis(ap=place[:, t:t + 1], axis=0),
                                             rows[t % 4][:, :], None).then_inc(sent[t % 4], 16)
            for i in range(4):
                pool.wait_ge(sent[i], 16 * (NT // 4))


def experts(nc, sem, W1, b1, W2, c_masks, expert_d, total_d, xs_d, ys_d):
    KC = HID // P
    with ExitStack() as ctx:
        def sb(name, shape, dt=F32):
            return ctx.enter_context(nc.sbuf_tensor("e_" + name, shape, dt))

        def ps(name, shape):
            return ctx.enter_context(nc.psum_tensor("e_" + name, shape, F32))

        masks = sb("masks", [P, 5, P])
        total = sb("total", [1, D])
        expert = sb("expert", [1, ET], I32)
        w1 = [sb(f"w1_{i}", [P, 2, HID]) for i in range(2)]
        w2 = [sb(f"w2_{i}", [P, KC, D]) for i in range(2)]
        bias = [sb(f"bias{i}", [P, KC]) for i in range(2)]
        xs = [sb(f"xs{i}", [P, D]) for i in range(2)]
        low, off = sb("low", [P, 2, KC]), sb("off", [P, 2, KC])
        xT = sb("xT", [P, 2, 2, P])
        hid = sb("hid", [P, 2, KC, P])
        ys = sb("ys", [P, 2, D])
        turn_ps = ps("turn_ps", [P, 4, P])
        hid_ps = [ps(f"hid_ps{i}", [P, KC, P]) for i in range(2)]
        out_ps = [ps(f"out_ps{i}", [P, 512]) for i in range(2)]
        held = sem("e_held")
        loaded = sem("e_loaded")
        tile_in, stored = ([sem(f"e_{w}{i}") for i in range(2)] for w in ("tile_in", "stored"))
        turned, xT_made, hid_made, low_made, relu_made, out_made, ys_made = (
            sem("e_turned"), sem("e_xT"), sem("e_hid"), sem("e_low"), sem("e_relu"), sem("e_out"), sem("e_ys"))

        def hold(eng, semaphore, value):
            eng.wait_ge(semaphore, value)
            eng.sem_inc(held, 1)

        block = ctx.enter_context(nc.Block())

        def steps(eng, step):
            for i in range(2):
                step(i, 0, i, True)
            with eng.Fori(1, ET // 2) as k:
                for i in range(2):
                    step(k * 2 + i, k, i, False)

        @block.sync
        def _(sp):
            sp.dma_start(masks[:, :, :], c_masks).then_inc(loaded, 16)
            sp.dma_start(total[:, :], total_d[:, :]).then_inc(loaded, 16)
            sp.dma_start(expert[:, :], expert_d[:, :]).then_inc(loaded, 16)
            hold(sp, loaded, 48)

            def load(s, k, i, first):
                if not first:
                    hold(sp, out_made, s - 1)
                e = sp.value_load(expert[0:1, bass.ds(s, 1)], min_val=0, max_val=E - 1)
                sp.dma_start(w1[i][:, :, :], view(W1.tensor, e * (D * HID), [[HID, P], [P * HID, 2], [1, HID]])).then_inc(tile_in[i], 16)
                sp.dma_start(w2[i][:, :, :], view(W2.tensor, e * (HID * D), [[D, P], [P * D, KC], [1, D]])).then_inc(tile_in[i], 16)
                sp.dma_start(bias[i][:, :], view(b1.tensor, e * HID, [[1, P], [P, KC]]),
                             allow_slow_non_contiguous=True).then_inc(tile_in[i], 16)
                sp.dma_start(xs[i][:, :], view(xs_d, s * (P * D), [[D, P], [1, D]])).then_inc(tile_in[i], 16)
            steps(sp, load)

        @block.scalar
        def _(act):
            def step(s, k, i, first):
                act.wait_ge(turned, s + 1)
                if not first:
                    act.wait_ge(hid_made, s - 1)
                nc.scalar.copy(xT[:, i, :, :], turn_ps[:, 2 * i:2 * i + 2, :]).then_inc(xT_made, 1)
                act.wait_ge(out_made, s + 1)
                if not first:
                    act.wait_ge(stored[i], k * 16)
                nc.scalar.copy(ys[:, i, :], out_ps[i][:, 0:D]).then_inc(ys_made, 1)
                act.wait_ge(ys_made, s + 1)
                act.dma_start(view(ys_d, s * (P * D), [[D, P], [1, D]]), ys[:, i, :]).then_inc(stored[i], 16)
            steps(act, step)
            for i in range(2):
                act.wait_ge(stored[i], 8 * ET)

        @block.vector
        def _(dve):
            def step(s, k, i, first):
                dve.wait_ge(tile_in[i], k * 64 + 64)
                if not first:
                    dve.wait_ge(relu_made, s - 1)
                nc.vector.tensor_scalar(off[:, i, :], bias[i][:, :], 0.0, -1.0, ALU.max, ALU.mult).then_inc(low_made, 1)
                nc.vector.tensor_scalar(low[:, i, :], bias[i][:, :], 0.0, None, ALU.min).then_inc(low_made, 1)
                dve.wait_ge(low_made, s * 2 + 2)
                dve.wait_ge(hid_made, s + 1)
                if not first:
                    dve.wait_ge(out_made, s - 1)
                for c in range(KC):
                    last = nc.vector.tensor_scalar(hid[:, i, c, :], hid_ps[i][:, c, :], low[:, i, c:c + 1],
                                                   off[:, i, c:c + 1], ALU.add, ALU.max)
                last.then_inc(relu_made, 1)
            steps(dve, step)

        @block.tensor
        def _(pe):
            pe.wait_ge(loaded, 48)

            def step(s, k, i, first):
                pe.wait_ge(tile_in[i], k * 64 + 64)
                if not first:
                    pe.wait_ge(xT_made, s - 1)
                for f in range(2):
                    last = nc.tensor.transpose(turn_ps[:, 2 * i + f, :], xs[i][:, f * P:(f + 1) * P], masks[:, 4, :])
                last.then_inc(turned, 1)
                pe.wait_ge(xT_made, s + 1)
                if not first:
                    pe.wait_ge(relu_made, s - 1)
                for c in range(KC):
                    for f in range(2):
                        last = nc.tensor.matmul(hid_ps[i][:, c, :], w1[i][:, f, c * P:(c + 1) * P], xT[:, i, f, :],
                                                start=(f == 0), stop=(f == 1))
                last.then_inc(hid_made, 1)
                pe.wait_ge(relu_made, s + 1)
                if not first:
                    pe.wait_ge(ys_made, s - 1)
                for c in range(KC):
                    nc.tensor.matmul(out_ps[i][:, 0:D], hid[:, i, c, :], w2[i][:, c, :], start=(c == 0), stop=False)
                nc.tensor.matmul(out_ps[i][:, 0:D], masks[0:1, 3, :], total[:, :], start=False, stop=True).then_inc(out_made, 1)
            steps(pe, step)


def finish(nc, sem, x2_d, sort_d, ys_d, out):
    with ExitStack() as ctx:
        def sb(name, shape, dt=F32):
            return ctx.enter_context(nc.sbuf_tensor("f_" + name, shape, dt))

        NB = 4
        place = sb("place", [P, NT], I32)
        y, x2, z = (sb(n, [P, NB, D]) for n in ("y", "x2", "z"))
        stats, mv, var, root, inv = (sb(n, [P, NB, k]) for n, k in
                                     (("stats", 6), ("mv", 2), ("var", 1), ("root", 1), ("inv", 1)))
        loaded = sem("f_loaded")
        y_in, x2_in, stored = ([sem(f"f_{w}{i}") for i in range(NB)] for w in ("y_in", "x2_in", "stored"))
        dve_s = Stages(sem("f_dve"), "stats", "mv", "var", "inv", "normal", "sum")
        rooted = sem("f_rooted")
        block = ctx.enter_context(nc.Block())

        @block.sync
        def _(sp):
            sp.dma_start(place[:, :], sort_d[:, :]).then_inc(loaded, 16)
            for t in range(NT):
                if t >= NB:
                    sp.wait_ge(dve_s.sem, dve_s.before(t - NB + 1))
                sp.dma_start(x2[:, t % NB, :], x2_d[t * P:(t + 1) * P, :]).then_inc(x2_in[t % NB], 16)

        @block.gpsimd
        def _(pool):
            pool.wait_ge(loaded, 16)
            for t in range(NT):
                if t >= NB:
                    pool.wait_ge(dve_s.sem, dve_s.before(t - NB + 1))
                nc.gpsimd.indirect_dma_start(y[:, t % NB, :], None, ys_d[:, :],
                                             bass.IndirectOffsetOnAxis(ap=place[:, t:t + 1], axis=0)).then_inc(y_in[t % NB], 16)

        @block.vector
        def _(dve):
            dve.sem_inc(dve_s.sem, 1)
            s = dve_s
            for t in range(NT):
                i = t % NB
                dve.wait_ge(y_in[i], 16 * (t // NB + 1))
                nc.vector.bn_stats(stats[:, i, :], y[:, i, :]).then_inc(s.sem, 1)
                dve.wait_ge(s.sem, s.after(t, "stats"))
                nc.vector.bn_aggr(mv[:, i, :], stats[:, i, :]).then_inc(s.sem, 1)
                dve.wait_ge(s.sem, s.after(t, "mv"))
                nc.vector.tensor_scalar_add(var[:, i, :], mv[:, i, 1:2], EPS).then_inc(s.sem, 1)
                dve.wait_ge(rooted, t + 1)
                nc.vector.reciprocal(inv[:, i, :], root[:, i, :]).then_inc(s.sem, 1)
                dve.wait_ge(s.sem, s.after(t, "inv"))
                if t >= NB:
                    dve.wait_ge(stored[i], 16 * (t // NB))
                nc.vector.tensor_scalar(z[:, i, :], y[:, i, :], mv[:, i, 0:1], inv[:, i, :], ALU.subtract, ALU.mult
                                        ).then_inc(s.sem, 1)
                dve.wait_ge(s.sem, s.after(t, "normal"))
                dve.wait_ge(x2_in[i], 16 * (t // NB + 1))
                nc.vector.tensor_tensor(z[:, i, :], z[:, i, :], x2[:, i, :], ALU.add).then_inc(s.sem, 1)

        @block.scalar
        def _(act):
            for t in range(NT):
                i = t % NB
                act.wait_ge(dve_s.sem, dve_s.after(t, "var"))
                nc.scalar.activation(root[:, i, :], var[:, i, :], ACT.Sqrt).then_inc(rooted, 1)
                act.wait_ge(dve_s.sem, dve_s.after(t, "sum"))
                act.dma_start(out[t * P:(t + 1) * P, :], z[:, i, :]).then_inc(stored[i], 16)
            for i in range(NB):
                act.wait_ge(stored[i], 16 * (NT // NB))


_INS = ['hidden_states', 'Wq', 'bq', 'Wk', 'bk', 'Wv', 'bv', 'Wo', 'bo', 'rel_embeddings', 'ln_scale', 'ln_bias']
_FFN = ['W1', 'b1', 'W2', 'b2', 'Wr', 'br']


def kernel(**inputs):
    import numpy as _np
    import concourse.bacc as _bacc
    from concourse import mybir as _mybir
    from concourse.bass_utils import run_bass_kernel_spmd as _run

    nc = _bacc.Bacc("TRN2", target_bir_lowering=False, num_devices=1)
    arrays, args = {}, []
    given = {"L0_attn_" + n: inputs["L0_attn_" + n] for n in _INS} | {"L0_ffn_" + n: inputs["L0_ffn_" + n] for n in _FFN}
    for name, value in (given | constants()).items():
        a = _np.ascontiguousarray(value)
        if name == "L0_attn_hidden_states":
            a = a.reshape(TOK, D)
        arrays[f"in_{name}_dram"] = a
        args.append(nc.dram_tensor(f"in_{name}_dram", a.shape, _mybir.dt.from_np(a.dtype), kind="ExternalInput").ap())
    args.append(nc.dram_tensor("out_0_dram", (TOK, D), F32, kind="ExternalOutput").ap())
    build(nc, *args)
    r = _run(nc, [arrays], core_ids=[0])
    return r.results[0]["out_0_dram"].reshape(B, S, D)
```

```python
from contextlib import ExitStack

import numpy as np

import concourse.bass as bass
from concourse import mybir
from concourse.alu_op_type import AluOpType as ALU

F32 = mybir.dt.float32
BF16 = mybir.dt.bfloat16
I32 = mybir.dt.int32
U32 = mybir.dt.uint32
ACT = mybir.ActivationFunctionType
AX = mybir.AxisListType

P = 128
B, S, D = 4, 1024, 256
TOK = B * S
NT = TOK // P
H, DH = 16, 16
N = B * H
QT = S // P
SPAN = 64
NBUCKET = 2 * SPAN
MAX_REL = 128
SCALE = float(1.0 / np.sqrt(np.float32(DH * 3)))
E, HID = 8, 1024
ET = NT + E
W3 = 3 * P
BAND = 2 * P - 1
PARTS = 3
QPARTS = (0, 1, 0, 0, 1, 2)
KPARTS = (0, 1, 1, 2, 0, 0)
KROWS = len(QPARTS) * DH
XROWS = KROWS + 9
EPS, EPS_ATT = 1e-5, 1e-7
ROUND = float(1.5 * 2 ** 23)


def buckets():
    rel = np.arange(-(S - 1), S)
    mid = SPAN // 2
    a = np.where((rel < mid) & (rel > -mid), mid - 1, np.abs(rel))
    ratio = np.log((a / mid).astype(np.float32)) / np.float32(np.log(np.float32((MAX_REL - 1) / mid)))
    far = np.ceil(ratio * np.float32(mid - 1)) + mid
    return rel, np.where(a <= mid, a, far * np.sign(rel)).astype(np.int64)


def constants():
    rel, bucket = buckets()
    of = dict(zip(rel.tolist(), bucket.tolist()))
    c2p = lambda r: min(max(of[r] + SPAN, 0), NBUCKET - 1)
    p2c = lambda r: min(max(-of[-r] + SPAN, 0), NBUCKET - 1)
    right, left = NBUCKET - 1, 0
    for r in range(P, S):
        assert (c2p(r), p2c(r), c2p(-r), p2c(-r)) == (right, right, left, left)
    pick = np.zeros((2, NBUCKET, 2 * P), np.float32)
    for v in range(BAND):
        for tab, r, table in ((0, P - 1 - v, c2p), (1, v - (P - 1), p2c)):
            pick[tab, table(r), v] += 1
            pick[tab, right if r >= 0 else left, v] -= 1
    pick[:, left, BAND] += 1
    pick[:, right, BAND] -= 1
    k, m = np.arange(P)[:, None], np.arange(P)[None, :]
    masks = np.zeros((P, 5, P), np.float32)
    masks[:, 0] = m > k
    masks[:, 1] = m < k
    masks[:, 2] = k < m
    masks[:, 3] = 1.0
    masks[:, 4] = k == m
    fold = np.zeros((P, DH), np.float32)
    fold[np.arange(P), np.arange(P) % 32 % DH] = np.arange(P) % 32 < DH
    side = np.zeros((P, 2, 8), np.float32)
    side[np.arange(P), :, np.arange(P) // DH] = 1.0
    steps = np.zeros((P, ET + 8), np.float32)
    steps[:] = np.concatenate([np.arange(ET), np.arange(8)])
    return dict(c_pick=pick, c_masks=masks, c_fold=fold, c_side=side, c_steps=steps)


def build(nc, x, Wq, bq, Wk, bk, Wv, bv, Wo, bo, rel_emb, ln_s, ln_b, W1, b1, W2, b2, Wr, br,
          c_pick, c_masks, c_fold, c_side, c_steps, out):
    ctx = ExitStack()
    with ctx:
        def sem(name):
            return ctx.enter_context(nc.semaphore(name))

        def dram(name, shape, dt=F32):
            return nc.dram_tensor(name, shape, dt)

        xn_d = dram("xn_d", [TOK, D])
        split_d = dram("split_d", [2, PARTS, N * DH, S], BF16)
        far_d = dram("far_d", [2, 2, N, PARTS, S], BF16)
        v_d = dram("v_d", [N, S, DH])
        pick_d = dram("pick_d", [2, PARTS, N * DH, 2 * P], BF16)
        skew_d = dram("skew_d", [2, 2, QT, P * W3 + 2 * P])
        posT_d = dram("posT_d", [P, 2 * 2 * 8])
        ctx_d = dram("ctx_d", [N, S, DH])
        x2_d = dram("x2_d", [TOK, D])
        xf_d = dram("xf_d", [TOK, D])
        xs_d = dram("xs_d", [ET * P, D])
        ys_d = dram("ys_d", [ET * P, D])

        spread(nc, sem, Wk, bk, rel_emb, c_pick, c_masks, c_side, pick_d, skew_d, posT_d)
        project(nc, sem, x, Wq, bq, Wk, bk, Wv, bv, c_masks, posT_d, xn_d, split_d, far_d, v_d)
        attend(nc, sem, c_masks, c_fold, split_d, far_d, v_d, pick_d, skew_d, xs_d, ctx_d)
        sort_d = dram("sort_d", [P, NT], I32)
        expert_d = dram("expert_d", [1, ET], I32)
        total_d = dram("total_d", [1, D])
        mix(nc, sem, x, xn_d, ctx_d, Wo, bo, ln_s, ln_b, Wr, br, c_masks, c_steps, x2_d, xf_d,
            sort_d, expert_d)
        constant_rows(nc, sem, b1, W2, b2, total_d)
        dispatch(nc, sem, xf_d, sort_d, xs_d)
        experts(nc, sem, W1, b1, W2, c_masks, expert_d, total_d, xs_d, ys_d)
        finish(nc, sem, x2_d, sort_d, ys_d, out)



def view(t, offset, dims):
    return bass.AP(tensor=t, offset=offset, ap=dims)


class Stages:

    def __init__(self, semaphore, *names):
        self.sem, self.names = semaphore, names

    def after(self, step, name):
        return step * len(self.names) + (self.names.index(name) + 2)

    def before(self, step):
        return step * len(self.names) + 1


def spread(nc, sem, Wk, bk, rel_emb, c_pick, c_masks, c_side, pick_d, skew_d, posT_d):
    with ExitStack() as ctx:
        def sb(name, shape, dt=F32):
            return ctx.enter_context(nc.sbuf_tensor("s_" + name, shape, dt))

        def ps(name, shape):
            return ctx.enter_context(nc.psum_tensor("s_" + name, shape, F32))

        wk = sb("wk", [P, 2, D])
        bk_row = sb("bk_row", [1, D])
        pick = sb("pick", [P, 2, 2 * P])
        masks = sb("masks", [P, 5, P])
        side = sb("side", [P, 2, 8])
        rel = sb("rel", [P, D])
        relT = sb("relT", [P, 2, P])
        pos = sb("pos", [P, D])
        posT = sb("posT", [P, 2, 2])
        far_w = sb("far_w", [P, 2, 2, 8])
        pick32 = sb("pick32", [P, 2, 2, 2 * P])
        rest = sb("rest", [P, 2, 2, 2 * P])
        part = sb("part", [P, PARTS, 2, 2, 2 * P], BF16)
        zeros = sb("zeros", [P, W3 + 2])
        relT_ps, pos_ps, posT_ps, pick_ps = (ps("relT_ps", [P, 2, P]), ps("pos_ps", [P, D]),
                                             ps("posT_ps", [P, 2, P]), ps("pick_ps", [P, 2, 2, 2 * P]))
        loaded, stored = sem("s_loaded"), sem("s_stored")
        pe_made, act_made, dve_made = sem("s_pe_made"), sem("s_act_made"), sem("s_dve_made")
        block = ctx.enter_context(nc.Block())

        @block.sync
        def _(sp):
            loads = [(wk[:, :, :], Wk.rearrange("(k p) n -> p k n", p=P)),
                     (bk_row[:, :], bk.rearrange("(a n) -> a n", a=1)),
                     (pick[:, 0, :], c_pick[0, :, :]), (pick[:, 1, :], c_pick[1, :, :]),
                     (masks[:, :, :], c_masks), (side[:, :, :], c_side), (rel[:, :], rel_emb)]
            assert len(loads) == 7
            for dst, src in loads:
                sp.dma_start(dst, src, allow_slow_non_contiguous=True).then_inc(loaded, 16)
            sp.wait_ge(dve_made, 1)
            sp.dma_start(view(skew_d, 0, [[W3 + 2, P], [P * (W3 + 2), 4 * QT], [1, W3 + 2]]),
                         zeros[:, :].unsqueeze(1).to_broadcast([P, 4 * QT, W3 + 2])).then_inc(stored, 16)
            sp.wait_ge(dve_made, 4)
            sp.wait_ge(act_made, 6)
            for b in range(B):
                for tab in range(2):
                    for n in range(PARTS):
                        sp.dma_start(pick_d[tab, n, b * D:(b + 1) * D, :].rearrange("(c p) v -> p c v", p=P),
                                     part[:, n, tab, :, :]).then_inc(stored, 16)
            sp.dma_start(posT_d[:, :], far_w[:, :, :, :].rearrange("p c s h -> p (c s h)")).then_inc(stored, 16)
            sp.wait_ge(stored, 16 * (1 + B * 2 * PARTS + 1))

        @block.tensor
        def _(pe):
            pe.wait_ge(loaded, 16 * 7)
            ident = masks[:, 4, :]
            for c in range(2):
                last = nc.tensor.transpose(relT_ps[:, c, :], rel[:, c * P:(c + 1) * P], ident)
            last.then_inc(pe_made, 1)
            pe.wait_ge(act_made, 1)
            for c in range(2):
                nc.tensor.matmul(pos_ps[:, :], relT[:, c, :], wk[:, c, :], start=(c == 0), stop=False)
            nc.tensor.matmul(pos_ps[:, :], masks[0:1, 3, :], bk_row[:, :], start=False, stop=True).then_inc(pe_made, 1)
            pe.wait_ge(act_made, 2)
            for c in range(2):
                nc.tensor.transpose(posT_ps[:, c, :], pos[:, c * P:(c + 1) * P], ident)
                for tab in range(2):
                    last = nc.tensor.matmul(pick_ps[:, tab, c, :], pos[:, c * P:(c + 1) * P], pick[:, tab, :],
                                            start=True, stop=True)
            last.then_inc(pe_made, 1)

        @block.scalar
        def _(act):
            act.wait_ge(pe_made, 1)
            nc.scalar.copy(relT[:, :, :], relT_ps[:, :, :]).then_inc(act_made, 1)
            act.wait_ge(pe_made, 2)
            nc.scalar.copy(pos[:, :], pos_ps[:, :]).then_inc(act_made, 1)
            act.wait_ge(pe_made, 3)
            nc.scalar.copy(posT[:, :, :], posT_ps[:, :, 0:P:P - 1]).then_inc(act_made, 1)
            for tab in range(2):
                last = nc.scalar.copy(pick32[:, tab, :, :], pick_ps[:, tab, :, :])
            last.then_inc(act_made, 1)
            act.wait_ge(act_made, 4)
            nc.scalar.copy(part[:, 0, :, :, :], pick32[:, :, :, :]).then_inc(act_made, 1)
            act.wait_ge(dve_made, 3)
            nc.scalar.copy(part[:, 1, :, :, :], rest[:, :, :, :]).then_inc(act_made, 1)

        @block.vector
        def _(dve):
            nc.vector.memset(zeros[:, :], 0.0).then_inc(dve_made, 1)
            dve.wait_ge(loaded, 16 * 7)
            dve.wait_ge(act_made, 3)
            for c in range(2):
                for s in range(2):
                    last = nc.vector.tensor_scalar(far_w[:, c, s, :], side[:, 0, :], posT[:, c, s:s + 1], None, ALU.mult)
            last.then_inc(dve_made, 1)
            dve.wait_ge(act_made, 5)
            nc.vector.tensor_tensor(rest[:, :, :, :], pick32[:, :, :, :], part[:, 0, :, :, :], ALU.subtract).then_inc(dve_made, 1)
            dve.wait_ge(act_made, 6)
            nc.vector.tensor_tensor(part[:, 2, :, :, :], rest[:, :, :, :], part[:, 1, :, :, :], ALU.subtract).then_inc(dve_made, 1)


def project(nc, sem, x, Wq, bq, Wk, bk, Wv, bv, c_masks, posT_d, xn_d, split_d, far_d, v_d):
    G = 512
    GT = G // P
    with ExitStack() as ctx:
        def sb(name, shape, dt=F32):
            return ctx.enter_context(nc.sbuf_tensor("p_" + name, shape, dt))

        def ps(name, shape):
            return ctx.enter_context(nc.psum_tensor("p_" + name, shape, F32))

        wq, wk, wv = (sb(n, [P, 2, D]) for n in ("wq", "wk", "wv"))
        bqk = sb("bqk", [P, 4])
        bv_b = sb("bv_b", [P, D])
        masks = sb("masks", [P, 5, P])
        far_w = sb("far_w", [P, 2, 16])
        xt, xn, v32 = (sb(n, [P, GT, D]) for n in ("xt", "xn", "v32"))
        stats = sb("stats", [P, GT, 6])
        mv = sb("mv", [P, GT, 2])
        std, rstd = sb("std", [P, GT]), sb("rstd", [P, GT])
        xT = sb("xT", [P, 2, G])
        qk32, rest = sb("qk32", [P, 4, G]), sb("rest", [P, 4, G])
        part = sb("part", [P, PARTS, 4, G], BF16)
        far32, far_rest = sb("far32", [16, 4, G]), sb("far_rest", [16, 4, G])
        far_part = sb("far_part", [16, PARTS, 4, G], BF16)
        big = ps("big", [P, 4, G])
        tr = ps("tr", [P, 2, G])
        v_ps = ps("v_ps", [P, GT, D])
        held = sem("p_held")
        loaded, xin, stored, xn_stored = sem("p_loaded"), sem("p_xin"), sem("p_stored"), sem("p_xn_stored")
        pe_s = Stages(sem("p_pe"), "turned", "qk", "v", "far")
        act_s = Stages(sem("p_act"), "root", "xT", "hi", "mid", "far32", "far_hi", "far_mid")
        dve_s = Stages(sem("p_dve"), "stats", "moments", "eps", "inverse", "normal", "qk", "v", "rest", "lo",
                       "far_rest", "far_lo")
        STORES = GT + 4 + 2 * 4

        def hold(eng, semaphore, value):
            eng.wait_ge(semaphore, value)
            eng.sem_inc(held, 1)

        block = ctx.enter_context(nc.Block())

        @block.sync
        def _(sp):
            loads = [(wq[:, :, :], Wq.rearrange("(k p) n -> p k n", p=P)),
                     (wk[:, :, :], Wk.rearrange("(k p) n -> p k n", p=P)),
                     (wv[:, :, :], Wv.rearrange("(k p) n -> p k n", p=P)),
                     (bqk[:, 0:2], bq.rearrange("(c p) -> p c", p=P)),
                     (bqk[:, 2:4], bk.rearrange("(c p) -> p c", p=P)),
                     (bv_b[:, :], view(bv.tensor, 0, [[0, P], [1, D]])),
                     (masks[:, :, :], c_masks), (far_w[:, :, :], posT_d[:, :].rearrange("p (c s) -> p c s", c=2))]
            assert len(loads) == 8
            sp.sem_inc(xn_stored, 16)
            sp.sem_inc(stored, 16)
            for dst, src in loads:
                sp.dma_start(dst, src, allow_slow_non_contiguous=True).then_inc(loaded, 16)
            with sp.Fori(0, B) as b:
                for g in range(2):
                    step = b * 2 + g
                    row = b * S + g * G
                    hold(sp, dve_s.sem, dve_s.before(step))
                    sp.dma_start(xt[:, :, :], view(x.tensor, row * D, [[D, P], [P * D, GT], [1, D]])).then_inc(xin, 16)
                    hold(sp, dve_s.sem, dve_s.after(step, "normal"))
                    sp.dma_start(view(xn_d, row * D, [[D, P], [P * D, GT], [1, D]]), xn[:, :, :]).then_inc(xn_stored, 16)
                    hold(sp, dve_s.sem, dve_s.after(step, "v"))
                    for t in range(GT):
                        sp.dma_start(view(v_d, b * (H * S * DH) + (g * G + t * P) * DH, [[DH, P], [S * DH, H], [1, DH]]),
                                     v32[:, t, :].rearrange("p (h d) -> p h d", h=H)).then_inc(stored, 16)
                    hold(sp, dve_s.sem, dve_s.after(step, "lo"))
                    for m in range(4):
                        at = (m // 2 * PARTS * (N * DH) + m % 2 * P) * S + g * G
                        sp.dma_start(view(split_d, b * (D * S) + at, [[S, P], [N * DH * S, PARTS], [1, G]]),
                                     part[:, :, m, :]).then_inc(stored, 16)
                    hold(sp, dve_s.sem, dve_s.after(step, "far_lo"))
                    for m in range(4):
                        for s in range(2):
                            at = ((m // 2 * 2 + s) * N + m % 2 * 8) * PARTS * S + g * G
                            sp.dma_start(view(far_d, b * (H * PARTS * S) + at, [[PARTS * S, 8], [S, PARTS], [1, G]]),
                                         far_part[s * 8:(s + 1) * 8, :, m, :]).then_inc(stored, 16)
            hold(sp, stored, TOK // G * (16 * STORES) + 16)
            hold(sp, xn_stored, TOK // G * 16 + 16)

        @block.vector
        def _(dve):
            dve.sem_inc(dve_s.sem, 1)
            dve.wait_ge(loaded, 16 * 8)
            with dve.Fori(0, TOK // G) as step:
                s = dve_s
                dve.wait_ge(xin, step * 16 + 16)
                for t in range(GT):
                    last = nc.vector.bn_stats(stats[:, t, :], xt[:, t, :])
                last.then_inc(s.sem, 1)
                dve.wait_ge(s.sem, s.after(step, "stats"))
                dve.sem_inc(held, 1)
                for t in range(GT):
                    last = nc.vector.bn_aggr(mv[:, t, :], stats[:, t, :])
                last.then_inc(s.sem, 1)
                dve.wait_ge(s.sem, s.after(step, "moments"))
                nc.vector.tensor_scalar_add(std[:, :], mv[:, :, 1], EPS).then_inc(s.sem, 1)
                dve.wait_ge(act_s.sem, act_s.after(step, "root"))
                nc.vector.reciprocal(rstd[:, :], std[:, :]).then_inc(s.sem, 1)
                dve.wait_ge(s.sem, s.after(step, "inverse"))
                dve.wait_ge(xn_stored, step * 16 + 16)
                for t in range(GT):
                    last = nc.vector.tensor_scalar(xn[:, t, :], xt[:, t, :], mv[:, t, 0:1], rstd[:, t:t + 1],
                                                   ALU.subtract, ALU.mult)
                last.then_inc(s.sem, 1)
                dve.wait_ge(stored, step * (16 * STORES) + 16)
                dve.wait_ge(pe_s.sem, pe_s.after(step, "qk"))
                for m in range(4):
                    last = nc.vector.tensor_scalar_add(qk32[:, m, :], big[:, m, :], bqk[:, m:m + 1])
                last.then_inc(s.sem, 1)
                dve.wait_ge(pe_s.sem, pe_s.after(step, "v"))
                nc.vector.tensor_tensor(v32[:, :, :], v_ps[:, :, :],
                                        bv_b[:, :].unsqueeze(1).to_broadcast([P, GT, D]), ALU.add).then_inc(s.sem, 1)
                dve.wait_ge(act_s.sem, act_s.after(step, "hi"))
                nc.vector.tensor_tensor(rest[:, :, :], qk32[:, :, :], part[:, 0, :, :], ALU.subtract).then_inc(s.sem, 1)
                dve.wait_ge(act_s.sem, act_s.after(step, "mid"))
                nc.vector.tensor_tensor(part[:, 2, :, :], rest[:, :, :], part[:, 1, :, :], ALU.subtract).then_inc(s.sem, 1)
                dve.wait_ge(act_s.sem, act_s.after(step, "far_hi"))
                nc.vector.tensor_tensor(far_rest[:, :, :], far32[:, :, :], far_part[:, 0, :, :], ALU.subtract).then_inc(s.sem, 1)
                dve.wait_ge(act_s.sem, act_s.after(step, "far_mid"))
                nc.vector.tensor_tensor(far_part[:, 2, :, :], far_rest[:, :, :], far_part[:, 1, :, :],
                                        ALU.subtract).then_inc(s.sem, 1)

        @block.scalar
        def _(act):
            act.sem_inc(act_s.sem, 1)
            with act.Fori(0, TOK // G) as step:
                s = act_s
                act.wait_ge(dve_s.sem, dve_s.after(step, "eps"))
                nc.scalar.activation(std[:, :], std[:, :], ACT.Sqrt).then_inc(s.sem, 1)
                act.wait_ge(pe_s.sem, pe_s.after(step, "turned"))
                nc.scalar.copy(xT[:, :, :], tr[:, :, :]).then_inc(s.sem, 1)
                act.wait_ge(dve_s.sem, dve_s.after(step, "qk"))
                nc.scalar.copy(part[:, 0, :, :], qk32[:, :, :]).then_inc(s.sem, 1)
                act.wait_ge(dve_s.sem, dve_s.after(step, "rest"))
                nc.scalar.copy(part[:, 1, :, :], rest[:, :, :]).then_inc(s.sem, 1)
                act.wait_ge(pe_s.sem, pe_s.after(step, "far"))
                nc.scalar.copy(far32[:, :, :], big[0:16, :, :]).then_inc(s.sem, 1)
                act.wait_ge(s.sem, s.after(step, "far32"))
                nc.scalar.copy(far_part[:, 0, :, :], far32[:, :, :]).then_inc(s.sem, 1)
                act.wait_ge(dve_s.sem, dve_s.after(step, "far_rest"))
                nc.scalar.copy(far_part[:, 1, :, :], far_rest[:, :, :]).then_inc(s.sem, 1)

        @block.tensor
        def _(pe):
            pe.sem_inc(pe_s.sem, 1)
            pe.wait_ge(loaded, 16 * 8)
            with pe.Fori(0, TOK // G) as step:
                s = pe_s
                pe.wait_ge(dve_s.sem, dve_s.after(step, "normal"))
                for t in range(GT):
                    for k in range(2):
                        last = nc.tensor.transpose(tr[:, k, t * P:(t + 1) * P], xn[:, t, k * P:(k + 1) * P], masks[:, 4, :])
                last.then_inc(s.sem, 1)
                pe.wait_ge(act_s.sem, act_s.after(step, "xT"))
                for m in range(4):
                    w = (wq, wk)[m // 2]
                    for k in range(2):
                        last = nc.tensor.matmul(big[:, m, :], w[:, k, m % 2 * P:(m % 2 + 1) * P], xT[:, k, :],
                                                start=(k == 0), stop=(k == 1))
                last.then_inc(s.sem, 1)
                for t in range(GT):
                    for k in range(2):
                        last = nc.tensor.matmul(v_ps[:, t, :], xT[:, k, t * P:(t + 1) * P], wv[:, k, :],
                                                start=(k == 0), stop=(k == 1))
                last.then_inc(s.sem, 1)
                pe.wait_ge(dve_s.sem, dve_s.after(step, "qk"))
                for m in range(4):
                    last = nc.tensor.matmul(big[0:16, m, :], far_w[:, m % 2, :], qk32[:, m, :], start=True, stop=True)
                last.then_inc(s.sem, 1)

def attend(nc, sem, c_masks, c_fold, split_d, far_d, v_d, pick_d, skew_d, xs_d, ctx_d):
    SLOT = P * W3 + 2 * P
    HATS = 18
    BUFS = 4
    with ExitStack() as ctx:
        def sb(name, shape, dt=F32):
            return ctx.enter_context(nc.sbuf_tensor("t_" + name, shape, dt))

        masks = sb("masks", [P, 5, P])
        fold = sb("fold", [P, DH])
        blank = sb("blank", [P, D])
        ones = sb("ones", [9, S], BF16)
        zeros = sb("zeros", [9, S], BF16)
        keys = [sb(f"keys{i}", [XROWS, S], BF16) for i in range(BUFS)]
        after = [sb(f"after{i}", [XROWS, S], BF16) for i in range(BUFS)]
        before = [sb(f"before{i}", [XROWS, S], BF16) for i in range(BUFS)]
        rows = [sb(f"rows{i}", [KROWS, 2, 2 * P], BF16) for i in range(BUFS)]
        vals = [sb(f"vals{i}", [P, QT, 32]) for i in range(2)]
        table = sb("table", [P, 2, 4, 2, 2 * P])
        side = [sb(f"side{i}", [P, 2, QT]) for i in range(2)]
        near = [sb(f"near{i}", [P, 2, QT, W3]) for i in range(2)]
        bent = sb("bent", [P, 4, P])
        probs = sb("probs", [P, 2, S])
        probsT = sb("probsT", [P, 2, QT, 4 * P])
        most = sb("most", [P, 2, 3])
        scaled = sb("scaled", [P, 2, 3])
        shift = sb("shift", [P, 2])
        total = sb("total", [P, 2, 2, 4])
        inverse = sb("inverse", [P, 2, 4])
        sumT = sb("sumT", [P, 4 * P])
        made = [sb(f"made{i}", [P, QT, DH]) for i in range(2)]
        scores_ps = [ctx.enter_context(nc.psum_tensor(f"t_scores{i}", [P, S], F32)) for i in range(2)]
        table_ps = ctx.enter_context(nc.psum_tensor("t_table_ps", [P, 2, 2 * P], F32))
        turn_ps = [ctx.enter_context(nc.psum_tensor(f"t_turn{i}", [P, 4, P], F32)) for i in range(2)]
        sum_ps = ctx.enter_context(nc.psum_tensor("t_sum_ps", [P, 4 * P], F32))

        held = sem("t_held")
        cleared = sem("t_cleared")
        const_in, set_up, rows_set = sem("t_const_in"), sem("t_set_up"), sem("t_rows_set")
        hats_in = [sem(f"t_hats_in{q}") for q in range(BUFS)]
        vals_in = sem("t_vals_in")
        table_made, table_kept = sem("t_table_made"), sem("t_table_kept")
        side_kept, bend_made, bent_in = sem("t_side_kept"), sem("t_bend_made"), sem("t_bent_in")
        skew_out = sem("t_skew_out")
        skew_in = [[sem(f"t_skew_in{i}{h}") for h in range(2)] for i in range(2)]
        scored, seen, shifted, expd = (sem("t_scored"), sem("t_seen"),
                                               sem("t_shifted"), sem("t_expd"))
        turned = [sem("t_turned0"), sem("t_turned1")]
        kept = [sem("t_kept0"), sem("t_kept1")]
        summed, sum_kept, folded, inverted, ctx_made = (
            sem("t_summed"), sem("t_sum_kept"), sem("t_folded"), sem("t_inverted"), sem("t_ctx_made"))
        ctx_out = [sem(f"t_ctx_out{i}") for i in range(2)]

        def hold(eng, semaphore, value):
            eng.wait_ge(semaphore, value)
            eng.sem_inc(held, 1)

        block = ctx.enter_context(nc.Block())

        def units(eng, unit):
            for q in range(BUFS):
                unit(0, q)
            with eng.Fori(1, N // BUFS - 1) as k:
                for q in range(BUFS):
                    unit(k, q)
            for q in range(BUFS):
                unit(N // BUFS - 1, q)

        def below(k, q, count):
            return isinstance(k, int) and BUFS * k + q < count

        def within(k, q):
            return not isinstance(k, int) or BUFS * k + q < N

        def window(t):
            lo, hi = max(t - 1, 0), min(t + 2, QT)
            return lo, hi, (lo - t + 1) * P, (hi - t + 1) * P

        @block.sync
        def _(sp):
            def load_unit(k, q, some):
                n, buf = k * BUFS + q, q % BUFS
                if some == 0 and not below(k, q, BUFS):
                    hold(sp, scored, n * 8 - 24)
                    hold(sp, table_made, n * 8 - 24)

                def stack(dst, tensor, at, part, wide, keys_side):
                    pairs = ((0, 1), (1, 2), (0, 0)) if keys_side else ((0, 1), (0, 0), (1, 2))
                    for j, (a, b) in enumerate(pairs):
                        sp.dma_start(dst[2 * DH * j:2 * DH * (j + 1)],
                                     view(tensor, at + a * part, [[(b - a) * part, 2], [wide, DH], [1, wide]])
                                     ).then_inc(hats_in[buf], 16)

                part, far, wide = N * DH * S, N * PARTS * S, 2 * P
                if some == 0:
                    stack(keys[buf], split_d, n * (DH * S) + PARTS * part, part, S, True)
                    stack(after[buf], split_d, n * (DH * S), part, S, False)
                    sp.dma_start(keys[buf][KROWS:KROWS + 6, :],
                                 view(far_d, n * (PARTS * S) + 2 * far, [[far, 2], [S, PARTS], [1, S]])
                                 ).then_inc(hats_in[buf], 16)
                elif some == 1:
                    stack(before[buf], split_d, n * (DH * S), part, S, False)
                    sp.dma_start(after[buf][KROWS + 6:XROWS, :],
                                 view(far_d, n * (PARTS * S) + far, [[S, PARTS], [1, S]])).then_inc(hats_in[buf], 16)
                    sp.dma_start(before[buf][KROWS + 6:XROWS, :],
                                 view(far_d, n * (PARTS * S), [[S, PARTS], [1, S]])).then_inc(hats_in[buf], 16)
                else:
                    part = N * DH * wide
                    for tab in range(2):
                        stack(rows[buf][:, tab, :], pick_d, n * (DH * wide) + tab * (PARTS * part), part, wide, tab == 0)

            def load_vals(k, q):
                n = k * BUFS + q
                if not below(k, q, 2):
                    hold(sp, summed, n * 2 - 2)
                sp.dma_start(vals[q % 2][:, :, 0:DH], view(v_d, n * (S * DH), [[DH, P], [P * DH, QT], [1, DH]])
                             ).then_inc(vals_in, 16)

            def skew_write(k, q, h):
                n, i = k * BUFS + q, q % 2
                hold(sp, table_kept, n * 8 + (4 * h + 4))
                if not below(k, q, 2):
                    hold(sp, skew_in[i][h], k * 64 + q // 2 * 32)
                for tab in range(2):
                    at = ((i * 2 + tab) * QT + 4 * h) * SLOT
                    sp.dma_start(view(skew_d, at + 1, [[W3, P], [SLOT, 4], [1, BAND]]),
                                 table[:, h, :, tab, 0:BAND]).then_inc(skew_out, 16)

            def skew_read(k, q, h):
                n, i = k * BUFS + q, q % 2
                if not below(k, q, 2):
                    hold(sp, scored, n * 8 - 8)
                    hold(sp, shifted, n * 8 - 8)
                hold(sp, skew_out, n * 64 + (h + 1) * 32)
                for tab in range(2):
                    at = ((i * 2 + tab) * QT + 4 * h) * SLOT
                    sp.dma_start(near[i][:, tab, 4 * h:4 * h + 4, :],
                                 view(skew_d, at, [[W3 - 1, P], [SLOT, 4], [1, W3]])).then_inc(skew_in[i][h], 16)

            def store(n, i):
                hold(sp, ctx_made, n * 2 + 2)
                sp.dma_start(view(ctx_d, n * (S * DH), [[DH, P], [P * DH, QT], [1, DH]]),
                             made[i][:, :, :]).then_inc(ctx_out[i], 16)

            sp.dma_start(masks[:, :, :], c_masks).then_inc(const_in, 16)
            sp.dma_start(fold[:, :], c_fold).then_inc(const_in, 16)
            hold(sp, set_up, 3)
            for i in range(BUFS):
                sp.dma_start(keys[i][KROWS + 6:XROWS, :], ones[0:3, :]).then_inc(rows_set, 16)
                sp.dma_start(after[i][KROWS:KROWS + 3, :], zeros[0:3, :]).then_inc(rows_set, 16)
                sp.dma_start(after[i][KROWS + 3:KROWS + 6, :], ones[0:3, :]).then_inc(rows_set, 16)
                sp.dma_start(before[i][KROWS:KROWS + 3, :], ones[0:3, :]).then_inc(rows_set, 16)
                sp.dma_start(before[i][KROWS + 3:KROWS + 6, :], zeros[0:3, :]).then_inc(rows_set, 16)
            for n in range(BUFS - 1):
                for some in range(3):
                    load_unit(0, n, some)
            for j in range(8):
                sp.dma_start(view(xs_d, j * (ET // 8 * P * D), [[D, P], [P * D, ET // 8], [1, D]]),
                             blank[:, :].unsqueeze(1).to_broadcast([P, ET // 8, D])).then_inc(cleared, 16)
            load_vals(0, 0)
            for h in range(2):
                skew_write(0, 0, h)
                skew_read(0, 0, h)

            def unit(k, q):
                if within(k, q + 1):
                    skew_write(k, q + 1, 0)
                if within(k, q + 3):
                    load_unit(k, q + 3, 0)
                if within(k, q + 1):
                    skew_read(k, q + 1, 0)
                    skew_write(k, q + 1, 1)
                if within(k, q + 3):
                    load_unit(k, q + 3, 1)
                if within(k, q + 1):
                    skew_read(k, q + 1, 1)
                    load_vals(k, q + 1)
                if within(k, q + 3):
                    load_unit(k, q + 3, 2)
                if not below(k, q, 1):
                    store(k * BUFS + (q - 1), (q - 1) % 2)
            units(sp, unit)
            store(N - 1, 1)
            for i in range(2):
                hold(sp, ctx_out[i], N * 8)
            hold(sp, cleared, 16 * 8)

        @block.tensor
        def _(pe):
            ident = masks[:, 4, :]

            def make_table(k, q, u):
                n, buf = k * BUFS + q, q % BUFS
                if u == 0:
                    pe.wait_ge(hats_in[buf], k * (HATS * 16) + (q // BUFS + 1) * (HATS * 16))
                if not (below(k, q, 1) and u == 0):
                    pe.wait_ge(table_kept, n * 8 + u)
                nc.tensor.matmul(table_ps[:, 0, :], after[buf][0:KROWS, u * P:(u + 1) * P], rows[buf][:, 0, :],
                                 start=True, stop=False)
                nc.tensor.matmul(table_ps[:, 1, :], keys[buf][0:KROWS, u * P:(u + 1) * P], rows[buf][:, 1, :],
                                 start=False, stop=True).then_inc(table_made, 1)

            def score(n, buf, t, first):
                i = buf % 2
                if not (first and t < 2):
                    pe.wait_ge(expd, n * 8 + (t - 1))
                ps = scores_ps[t % 2]
                lo, hi, _, _ = window(t)
                edge = (t + 1) * P
                cuts = sorted({0, 512, S, edge})
                for a, z in zip(cuts[:-1], cuts[1:]):
                    q = after[buf] if z <= edge else before[buf]
                    more = any(j * P // 512 == a // 512 for j in range(lo, hi))
                    nc.tensor.matmul(ps[:, a:z], q[:, t * P:(t + 1) * P], keys[buf][:, a:z],
                                     start=a % 512 == 0, stop=z % 512 == 0 and not more)
                pe.wait_ge(bent_in, n * 2 + (1 if t < 3 else 2))
                for j in range(lo, hi):
                    final = nc.tensor.matmul(ps[:, j * P:(j + 1) * P],
                                             near[i][:, 1, j, (t - j + 1) * P:(t - j + 2) * P], ident,
                                             start=False, stop=(j == hi - 1 or (j + 1) * P == 512), is_transpose=True)
                final.then_inc(scored, 1)

            def turn(n, t, first):
                pe.wait_ge(expd, n * 8 + (t + 1))
                for h in range(2):
                    if not (first and t == 0):
                        pe.wait_ge(kept[h], n * 8 + t)
                    for j in range(4):
                        final = nc.tensor.transpose(turn_ps[h][:, j, :], probs[:, t % 2, (4 * h + j) * P:(4 * h + j + 1) * P], ident)
                    final.then_inc(turned[h], 1)

            def weigh(n, i, half, part, first):
                if part == 0:
                    if half == 0:
                        pe.wait_ge(vals_in, n * 16 + 16)
                    for h in range(2):
                        pe.wait_ge(kept[h], n * 8 + (4 * half + 4))
                    if not (first and half == 0):
                        pe.wait_ge(ctx_made, n * 2 + half)
                for j in range(4 * part, 4 * part + 4):
                    g = j % 4 * 32
                    final = nc.tensor.matmul(sum_ps[g:g + 32, :], vals[i][:, j, :], probsT[:, half, j, :],
                                             start=(part == 0), stop=(part == 1), skip_group_check=True)
                if part == 1:
                    final.then_inc(summed, 1)

            def add_groups(n, half):
                pe.wait_ge(sum_kept, n * 2 + (half + 1))
                for q in range(4):
                    final = nc.tensor.matmul(sum_ps[:, q * DH:(q + 1) * DH], sumT[:, q * P:(q + 1) * P], fold[:, :],
                                             start=True, stop=True)
                final.then_inc(folded, 1)

            pe.wait_ge(const_in, 32)
            pe.wait_ge(rows_set, 16 * 5 * BUFS)
            pe.wait_ge(set_up, 5)
            for j in range(QT + 4):
                make_table(0, j // QT, j % QT)

            def unit(k, q):
                n, i, first = k * BUFS + q, q % 2, below(k, q, 1)
                for t in range(QT):
                    score(n, q, t, first)
                    if t % 4 == 1 and not first:
                        add_groups(n - 1, t // 4)
                    if t >= 2:
                        turn(n, t - 2, first)
                    elif not first:
                        turn(n - 1, QT - 2 + t, False)
                    ahead = q + 1 + t // 4
                    if within(k, ahead):
                        make_table(k, ahead, (t + 4) % QT)
                    if t in (2, 3) and not first:
                        weigh(n - 1, 1 - i, 1, t - 2, False)
                    if t in (6, 7):
                        weigh(n, i, 0, t - 6, first)
            units(pe, unit)
            turn(N - 1, QT - 2, False)
            add_groups(N - 1, 0)
            turn(N - 1, QT - 1, False)
            for part in range(2):
                weigh(N - 1, 1, 1, part, False)
            add_groups(N - 1, 1)

        @block.vector
        def _(dve):
            def row_max(n, i, t, first):
                ps = scores_ps[t % 2]
                lo, hi, a, z = window(t)
                dve.wait_ge(bent_in, n * 2 + (1 if t < 4 else 2))
                dve.wait_ge(scored, n * 8 + (t + 1))
                many = 1
                for u, v in ((0, lo * P), (hi * P, S)):
                    if v > u:
                        nc.vector.tensor_reduce(most[:, t % 2, many:many + 1], ps[:, u:v], AX.X, ALU.max)
                        many += 1
                nc.vector.tensor_tensor_reduce(ps[:, lo * P:hi * P], ps[:, lo * P:hi * P], near[i][:, 0, t, a:z],
                                               1.0, -3.0e38, ALU.add, ALU.max, accum_out=most[:, t % 2, 0:1]
                                               ).then_inc(seen, 1)
                dve.wait_ge(seen, n * 8 + (t + 1))
                nc.vector.tensor_scalar(scaled[:, t % 2, 0:many], most[:, t % 2, 0:many], -SCALE, None, ALU.mult, ALU.min,
                                        accum_out=shift[:, t % 2:t % 2 + 1]).then_inc(shifted, 1)

            def keep(n, t, first):
                dve.wait_ge(turned[0], n * 8 + (t + 1))
                if not (first and t < 4):
                    dve.wait_ge(summed, n * 2 + (t // 4 - 1))
                nc.vector.tensor_copy(probsT[:, t // 4, 0:4, t % 4 * P:(t % 4 + 1) * P],
                                      turn_ps[0][:, :, :]).then_inc(kept[0], 1)

            def divide(k, q, half):
                n, i = k * BUFS + q, q % 2
                nc.vector.reciprocal(inverse[:, half, :], total[:, i, half, :]).then_inc(inverted, 1)
                dve.wait_ge(inverted, n * 2 + (half + 1))
                dve.wait_ge(folded, n * 2 + (half + 1))
                if not below(k, q, 2):
                    dve.wait_ge(ctx_out[i], k * 32 + q // 2 * 16)
                nc.vector.tensor_tensor(made[i][:, 4 * half:4 * half + 4, :],
                                        sum_ps[:, 0:4 * DH].rearrange("p (q d) -> p q d", q=4),
                                        inverse[:, half, :].unsqueeze(2).to_broadcast([P, 4, DH]),
                                        ALU.mult).then_inc(ctx_made, 1)

            nc.vector.memset(blank[:, :], 0.0).then_inc(set_up, 1)
            nc.vector.memset(ones[:, :], 1.0).then_inc(set_up, 1)
            nc.vector.memset(zeros[:, :], 0.0).then_inc(set_up, 1)
            for i in range(2):
                nc.vector.memset(vals[i][:, :, DH:32], 0.0).then_inc(set_up, 1)

            def unit(k, q):
                n, i, first = k * BUFS + q, q % 2, below(k, q, 1)
                for t in range(QT):
                    row_max(n, i, t, first)
                    if t >= 2:
                        keep(n, t - 2, first)
                    elif not first:
                        keep(n - 1, QT - 2 + t, False)
                    if t % 4 == 1 and not first:
                        divide(k, q - 1, t // 4)
            units(dve, unit)
            keep(N - 1, QT - 2, False)
            divide(N // BUFS - 1, BUFS - 1, 0)
            keep(N - 1, QT - 1, False)
            divide(N // BUFS - 1, BUFS - 1, 1)

        @block.scalar
        def _(act):
            def keep_table(k, q, u):
                n = k * BUFS + q
                act.wait_ge(table_made, n * 8 + (u + 1))
                if u % 4 == 0 and not below(k, q, 1):
                    h = u // 4
                    act.wait_ge(skew_out, (n * 2 + (h - 1)) * 32)
                    act.wait_ge(side_kept, n * 2 + (h - 1))
                nc.scalar.copy(table[:, u // 4, u % 4, :, :], table_ps[:, :, :]).then_inc(table_kept, 1)

            def exponent(n, t, i, early):
                act.wait_ge(shifted, n * 8 + (t + 1))
                if not (isinstance(n, int) and n == 0 and t < 2):
                    act.wait_ge(turned[1], n * 8 + (t - 1))
                if t % 4 == 0 and not early:
                    act.wait_ge(ctx_made, n * 2 + (t // 4 - 3))
                nc.scalar.activation(probs[:, t % 2, :], scores_ps[t % 2][:, :], ACT.Exp, bias=shift[:, t % 2:t % 2 + 1],
                                     scale=SCALE, accum_out=total[:, i, t // 4, t % 4:t % 4 + 1]).then_inc(expd, 1)

            def keep(n, t, first):
                act.wait_ge(turned[1], n * 8 + (t + 1))
                if not (first and t < 4):
                    act.wait_ge(summed, n * 2 + (t // 4 - 1))
                nc.scalar.copy(probsT[:, t // 4, 4:8, t % 4 * P:(t % 4 + 1) * P], turn_ps[1][:, :, :]).then_inc(kept[1], 1)

            def keep_sum(n, half, first):
                act.wait_ge(summed, n * 2 + (half + 1))
                if not (first and half == 0):
                    act.wait_ge(folded, n * 2 + half)
                nc.scalar.copy(sumT[:, :], sum_ps[:, :]).then_inc(sum_kept, 1)

            for j in range(QT + 4):
                keep_table(0, j // QT, j % QT)

            def unit(k, q):
                n, i, first = k * BUFS + q, q % 2, below(k, q, 1)
                for t in range(QT):
                    if t >= 2:
                        keep(n, t - 2, first)
                    elif not first:
                        keep(n - 1, QT - 2 + t, False)
                    if t % 4 == 0 and not first:
                        keep_sum(n - 1, t // 4, below(k, q, 2))
                    exponent(n, t, i, below(k, q, 2))
                    ahead = q + 1 + t // 4
                    if within(k, ahead):
                        keep_table(k, ahead, (t + 4) % QT)
            units(act, unit)
            keep(N - 1, QT - 2, False)
            keep_sum(N - 1, 0, False)
            keep(N - 1, QT - 1, False)
            keep_sum(N - 1, 1, False)

        @block.gpsimd
        def _(pool):
            def bend(k, q):
                n, i = k * BUFS + q, q % 2
                for h in range(2):
                    pool.wait_ge(table_kept, n * 8 + (4 * h + 4))
                    column = table[:, h, :, :, BAND]
                    nc.gpsimd.tensor_tensor(side[i][:, :, 4 * h:4 * h + 4].rearrange("p a t -> p t a"),
                                            column, masks[:, 3, 0:8].rearrange("p (t a) -> p t a", a=2),
                                            ALU.mult).then_inc(side_kept, 1)
                    pool.wait_ge(side_kept, n * 2 + (h + 1))
                    pool.wait_ge(skew_in[i][h], k * 64 + (q // 2 + 1) * 32)
                    pool.wait_ge(bent_in, n * 2 + h)
                    for tab in range(2):
                        nc.gpsimd.tensor_tensor(bent[:, :, :], masks[:, tab, :].unsqueeze(1).to_broadcast([P, 4, P]),
                                                side[i][:, tab, 4 * h:4 * h + 4].unsqueeze(2).to_broadcast([P, 4, P]),
                                                ALU.mult).then_inc(bend_made, 1)
                        pool.wait_ge(bend_made, n * 6 + (3 * h + 2 * tab + 1))
                        diag = near[i][:, tab, 4 * h:4 * h + 4, P:2 * P]
                        nc.gpsimd.tensor_tensor(diag, diag, bent[:, :, :], ALU.add
                                                ).then_inc((bend_made, bent_in)[tab], 1)
                        if tab == 0:
                            pool.wait_ge(bend_made, n * 6 + (3 * h + 2))

            pool.wait_ge(const_in, 32)
            bend(0, 0)

            def unit(k, q):
                if within(k, q + 1):
                    bend(k, q + 1)
            units(pool, unit)


def mix(nc, sem, x, xn_d, ctx_d, Wo, bo, ln_s, ln_b, Wr, br, c_masks, c_steps, x2_d, xf_d, sort_d, expert_d):
    with ExitStack() as ctx:
        def sb(name, shape, dt=F32):
            return ctx.enter_context(nc.sbuf_tensor("m_" + name, shape, dt))

        def ps(name, shape):
            return ctx.enter_context(nc.psum_tensor("m_" + name, shape, F32))

        wo, wr = sb("wo", [P, 2, D]), sb("wr", [P, 2, E])
        bo_b, ls_b, lb_b, br_b = sb("bo_b", [P, D]), sb("ls_b", [P, D]), sb("lb_b", [P, D]), sb("br_b", [P, E])
        masks, steps = sb("masks", [P, 5, P]), sb("steps", [P, ET + 8])
        ctx_in, xt, xn = sb("ctx_in", [P, H, DH]), sb("xt", [P, D]), sb("xn", [P, D])
        turned, xfT = sb("turned", [P, 2, P]), sb("xfT", [P, 2, P])
        y0, y1, y2, y3, y4, y5, y6, x2, xf = (sb(f"y{i}", [P, D]) for i in range(9))
        logits, top, index = sb("logits", [P, E]), sb("top", [P, E]), sb("index", [P, E], U32)
        choice = sb("choice", [P, NT])
        turn_ps, out_ps, logit_ps = ps("turn_ps", [P, 4, P]), ps("out_ps", [P, 512]), ps("logit_ps", [P, 512])
        before_ps, count_ps = ps("before_ps", [P, 512]), ps("count_ps", [P, 512])
        held = sem("m_held")
        loaded, tile_in, stored = sem("m_loaded"), sem("m_tile_in"), sem("m_stored")
        norms = [[sb(f"{w}{i}", [P, n]) for w, n in (("stats", 6), ("mv", 2), ("var", 1), ("root", 1), ("inv", 1))]
                 for i in range(3)]
        norm_stages = [f"{w}{i}" for i in range(3) for w in ("stats", "mv", "var", "inv", "out")]
        dve_s = Stages(sem("m_dve"), "residual", "bias", *norm_stages[:5], "scaled", "shifted", *norm_stages[5:10],
                       "x2", *norm_stages[10:], "logits", "top", "index", "choice")
        act_s = Stages(sem("m_act"), "turned", "root0", "root1", "root2", "xfT")
        pe_s = Stages(sem("m_pe"), "turned", "out", "xfT", "logits")
        SORTED = 21
        sorting = sem("m_sorting")
        sorted_pe = sem("m_sorted_pe")

        def hold(eng, semaphore, value):
            eng.wait_ge(semaphore, value)
            eng.sem_inc(held, 1)

        block = ctx.enter_context(nc.Block())

        hot = sb("hot", [P, NT, E])
        scan = [sb(f"scan{i}", [P, NT, E]) for i in range(2)]
        counts, base = sb("counts", [P, NT, E]), sb("base", [P, E])
        tiles = sb("tiles", [P, E])
        ends = [sb(f"ends{i}", [P, E]) for i in range(2)]
        places, chosen = sb("places", [P, NT, E]), sb("chosen", [P, NT, E])
        place, place_i = sb("place", [P, NT]), sb("place_i", [P, NT], I32)
        behind, expert, expert_c, expert_i = (sb("behind", [P, ET, E]), sb("expert", [P, ET]), sb("expert_c", [P, ET]),
                                              sb("expert_i", [P, ET], I32))

        @block.sync
        def _(sp):
            def row(src, n):
                return view(src.tensor, 0, [[0, P], [1, n]])
            loads = [(wo[:, :, :], Wo.rearrange("(k p) n -> p k n", p=P)),
                     (wr[:, :, :], Wr.rearrange("(k p) n -> p k n", p=P)),
                     (bo_b[:, :], row(bo, D)), (ls_b[:, :], row(ln_s, D)), (lb_b[:, :], row(ln_b, D)),
                     (br_b[:, :], row(br, E)), (masks[:, :, :], c_masks), (steps[:, :], c_steps)]
            assert len(loads) == 8
            sp.sem_inc(stored, 16)
            for dst, src in loads:
                sp.dma_start(dst, src, allow_slow_non_contiguous=True).then_inc(loaded, 16)
            with sp.Fori(0, B) as b:
                for q in range(QT):
                    step = b * QT + q
                    row0 = b * S + q * P
                    hold(sp, dve_s.sem, dve_s.before(step))
                    sp.dma_start(ctx_in[:, :, :], view(ctx_d, b * (H * S * DH) + q * P * DH,
                                                       [[DH, P], [S * DH, H], [1, DH]])).then_inc(tile_in, 16)
                    sp.dma_start(xt[:, :], view(x.tensor, row0 * D, [[D, P], [1, D]])).then_inc(tile_in, 16)
                    sp.dma_start(xn[:, :], view(xn_d, row0 * D, [[D, P], [1, D]])).then_inc(tile_in, 16)
                    hold(sp, dve_s.sem, dve_s.after(step, "out2"))
                    sp.dma_start(view(x2_d, row0 * D, [[D, P], [1, D]]), x2[:, :]).then_inc(stored, 16)
                    sp.dma_start(view(xf_d, row0 * D, [[D, P], [1, D]]), xf[:, :]).then_inc(stored, 16)
            hold(sp, sorting, SORTED)
            sp.dma_start(sort_d[:, :], place_i[:, :]).then_inc(stored, 16)
            sp.dma_start(expert_d[:, :], expert_i[0:1, :]).then_inc(stored, 16)
            hold(sp, stored, 16 * (2 * NT + 3))

        @block.vector
        def _(dve):
            dve.sem_inc(dve_s.sem, 1)
            s = dve_s
            dve.wait_ge(loaded, 16 * 8)
            with dve.Fori(0, NT) as step:
                def own(name):
                    dve.wait_ge(s.sem, s.after(step, name))

                def norm(i, src, dst, eps):
                    stats, mv, var, root, inv = norms[i]
                    nc.vector.bn_stats(stats[:, :], src[:, :]).then_inc(s.sem, 1)
                    own(f"stats{i}")
                    dve.sem_inc(held, 1)
                    nc.vector.bn_aggr(mv[:, :], stats[:, :]).then_inc(s.sem, 1)
                    own(f"mv{i}")
                    nc.vector.tensor_scalar_add(var[:, :], mv[:, 1:2], eps).then_inc(s.sem, 1)
                    dve.wait_ge(act_s.sem, act_s.after(step, f"root{i}"))
                    nc.vector.reciprocal(inv[:, :], root[:, :]).then_inc(s.sem, 1)
                    own(f"inv{i}")
                    nc.vector.tensor_scalar(dst[:, :], src[:, :], mv[:, 0:1], inv[:, :], ALU.subtract, ALU.mult
                                            ).then_inc(s.sem, 1)
                    own(f"out{i}")

                dve.wait_ge(tile_in, step * 48 + 48)
                dve.wait_ge(pe_s.sem, pe_s.after(step, "out"))
                nc.vector.tensor_tensor(y0[:, :], out_ps[:, 0:D], xn[:, :], ALU.add).then_inc(s.sem, 1)
                own("residual")
                nc.vector.tensor_tensor(y1[:, :], y0[:, :], bo_b[:, :], ALU.add).then_inc(s.sem, 1)
                own("bias")
                norm(0, y1, y2, EPS_ATT)
                nc.vector.tensor_tensor(y3[:, :], y2[:, :], ls_b[:, :], ALU.mult).then_inc(s.sem, 1)
                own("scaled")
                nc.vector.tensor_tensor(y4[:, :], y3[:, :], lb_b[:, :], ALU.add).then_inc(s.sem, 1)
                own("shifted")
                norm(1, y4, y5, EPS)
                dve.wait_ge(stored, step * 32 + 16)
                nc.vector.tensor_tensor(x2[:, :], xt[:, :], y5[:, :], ALU.add).then_inc(s.sem, 1)
                own("x2")
                norm(2, x2, xf, EPS)
                dve.wait_ge(pe_s.sem, pe_s.after(step, "logits"))
                nc.vector.tensor_tensor(logits[:, :], logit_ps[:, 0:E], br_b[:, :], ALU.add).then_inc(s.sem, 1)
                own("logits")
                dve.sem_inc(held, 1)
                nc.vector.max(top[:, :], logits[:, :]).then_inc(s.sem, 1)
                own("top")
                dve.sem_inc(held, 1)
                nc.vector.max_index(index[:, :], top[:, :], logits[:, :]).then_inc(s.sem, 1)
                own("index")
                nc.vector.tensor_copy(choice[:, bass.ts(step, 1)], index[:, 0:1]).then_inc(s.sem, 1)
            count = [0]

            def link(instruction):
                instruction.then_inc(sorting, 1)
                count[0] += 1
                dve.wait_ge(sorting, count[0])

            dve.wait_ge(s.sem, s.before(NT))
            link(nc.vector.tensor_tensor(hot[:, :, :], choice[:, :].unsqueeze(2).to_broadcast([P, NT, E]),
                                         steps[:, ET:ET + E].unsqueeze(1).to_broadcast([P, NT, E]), ALU.is_equal))
            dve.wait_ge(sorted_pe, 1)
            link(nc.vector.tensor_copy(counts[:, :, :], count_ps[:, 0:NT * E].rearrange("p (t e) -> p t e", e=E)))
            src, k = counts, 0
            d = 1
            while d < NT:
                dst = scan[k % 2]
                nc.vector.tensor_copy(dst[:, 0:d, :], src[:, 0:d, :])
                link(nc.vector.tensor_tensor(dst[:, d:NT, :], src[:, d:NT, :], src[:, 0:NT - d, :], ALU.add))
                src, k, d = dst, k + 1, 2 * d
            upto = src
            link(nc.vector.tensor_scalar(tiles[:, :], upto[:, NT - 1, :], 1.0 / P, 0.5 - 1.0 / (2 * P), ALU.mult, ALU.add))
            link(nc.vector.tensor_scalar(base[:, :], tiles[:, :], ROUND, -ROUND, ALU.add, ALU.add))
            link(nc.vector.tensor_copy(tiles[:, :], base[:, :]))
            src, k, d = tiles, 0, 1
            while d < E:
                dst = ends[k % 2]
                nc.vector.tensor_copy(dst[:, 0:d], src[:, 0:d])
                link(nc.vector.tensor_tensor(dst[:, d:E], src[:, d:E], src[:, 0:E - d], ALU.add))
                src, k, d = dst, k + 1, 2 * d
            end = src
            nc.vector.tensor_tensor(behind[:, :, :], steps[:, 0:ET].unsqueeze(2).to_broadcast([P, ET, E]),
                                    end[:, :].unsqueeze(1).to_broadcast([P, ET, E]), ALU.is_ge)
            link(nc.vector.tensor_tensor(base[:, :], end[:, :], tiles[:, :], ALU.subtract))
            nc.vector.tensor_reduce(expert[:, :], behind[:, :, :], AX.X, ALU.add)
            link(nc.vector.tensor_tensor(places[:, :, :], upto[:, :, :], counts[:, :, :], ALU.subtract))
            link(nc.vector.tensor_tensor(chosen[:, :, :], places[:, :, :],
                                         before_ps[:, 0:NT * E].rearrange("p (t e) -> p t e", e=E), ALU.add))
            link(nc.vector.tensor_scalar(tiles[:, :], base[:, :], float(P), None, ALU.mult))
            nc.vector.tensor_scalar_min(expert_c[:, :], expert[:, :], float(E - 1))
            link(nc.vector.tensor_tensor(places[:, :, :], chosen[:, :, :],
                                         tiles[:, :].unsqueeze(1).to_broadcast([P, NT, E]), ALU.add))
            nc.vector.tensor_copy(expert_i[:, :], expert_c[:, :])
            link(nc.vector.tensor_tensor(chosen[:, :, :], places[:, :, :], hot[:, :, :], ALU.mult))
            link(nc.vector.tensor_reduce(place[:, :], chosen[:, :, :], AX.X, ALU.add))
            link(nc.vector.tensor_copy(place_i[:, :], place[:, :]))
            assert count[0] == SORTED, count[0]

        @block.scalar
        def _(act):
            act.sem_inc(act_s.sem, 1)
            with act.Fori(0, NT) as step:
                act.wait_ge(pe_s.sem, pe_s.after(step, "turned"))
                nc.scalar.copy(turned[:, :, :], turn_ps[:, 0:2, :]).then_inc(act_s.sem, 1)
                for i in range(3):
                    act.wait_ge(dve_s.sem, dve_s.after(step, f"var{i}"))
                    nc.scalar.activation(norms[i][3][:, :], norms[i][2][:, :], ACT.Sqrt).then_inc(act_s.sem, 1)
                act.wait_ge(pe_s.sem, pe_s.after(step, "xfT"))
                nc.scalar.copy(xfT[:, :, :], turn_ps[:, 2:4, :]).then_inc(act_s.sem, 1)

        @block.tensor
        def _(pe):
            pe.sem_inc(pe_s.sem, 1)
            pe.wait_ge(loaded, 16 * 8)
            ident = masks[:, 4, :]
            with pe.Fori(0, NT) as step:
                pe.wait_ge(tile_in, step * 48 + 48)
                pe.wait_ge(act_s.sem, act_s.before(step))
                for k in range(2):
                    last = nc.tensor.transpose(turn_ps[:, k, :], ctx_in[:, :, :].rearrange("p h d -> p (h d)")[:, k * P:(k + 1) * P], ident)
                last.then_inc(pe_s.sem, 1)
                pe.wait_ge(act_s.sem, act_s.after(step, "turned"))
                for k in range(2):
                    last = nc.tensor.matmul(out_ps[:, 0:D], turned[:, k, :], wo[:, k, :], start=(k == 0), stop=(k == 1))
                last.then_inc(pe_s.sem, 1)
                pe.wait_ge(dve_s.sem, dve_s.after(step, "out2"))
                for k in range(2):
                    last = nc.tensor.transpose(turn_ps[:, 2 + k, :], xf[:, k * P:(k + 1) * P], ident)
                last.then_inc(pe_s.sem, 1)
                pe.wait_ge(act_s.sem, act_s.after(step, "xfT"))
                for k in range(2):
                    last = nc.tensor.matmul(logit_ps[:, 0:E], xfT[:, k, :], wr[:, k, :], start=(k == 0), stop=(k == 1))
                last.then_inc(pe_s.sem, 1)
            pe.wait_ge(sorting, 1)
            hot2 = hot[:, :, :].rearrange("p t e -> p (t e)")
            nc.tensor.matmul(before_ps[:, 0:NT * E], masks[:, 2, :], hot2, start=True, stop=True)
            nc.tensor.matmul(count_ps[:, 0:NT * E], masks[:, 3, :], hot2, start=True, stop=True).then_inc(sorted_pe, 1)


def constant_rows(nc, sem, b1, W2, b2, total_d):
    KC = HID // P
    with ExitStack() as ctx:
        w2 = [ctx.enter_context(nc.sbuf_tensor(f"c_w2_{i}", [P, KC, D], F32)) for i in range(2)]
        b1_sb = ctx.enter_context(nc.sbuf_tensor("c_b1", [P, E, KC], F32))
        r1 = ctx.enter_context(nc.sbuf_tensor("c_r1", [P, E, KC], F32))
        b2_sb = ctx.enter_context(nc.sbuf_tensor("c_b2", [E, D], F32))
        ones = ctx.enter_context(nc.sbuf_tensor("c_ones", [E, 1], F32))
        row = ctx.enter_context(nc.sbuf_tensor("c_row", [1, D], F32))
        row_ps = ctx.enter_context(nc.psum_tensor("c_row_ps", [1, 512], F32))
        loaded, made, used, stored = sem("c_loaded"), sem("c_made"), sem("c_used"), sem("c_stored")
        w2_in = [sem("c_w2_in0"), sem("c_w2_in1")]
        block = ctx.enter_context(nc.Block())

        @block.sync
        def _(sp):
            sp.dma_start(b1_sb[:, :, :], b1.rearrange("e (c p) -> p e c", p=P),
                         allow_slow_non_contiguous=True).then_inc(loaded, 16)
            sp.dma_start(b2_sb[:, :], b2).then_inc(loaded, 16)
            for e in range(E):
                if e >= 2:
                    sp.wait_ge(used, e - 1)
                sp.dma_start(w2[e % 2][:, :, :], W2[e, :, :].rearrange("(c p) n -> p c n", p=P)).then_inc(w2_in[e % 2], 16)
            sp.wait_ge(made, 3)
            sp.dma_start(total_d[:, :], row[:, :]).then_inc(stored, 16)
            sp.wait_ge(stored, 16)

        @block.vector
        def _(dve):
            nc.vector.memset(ones[:, :], 1.0).then_inc(made, 1)
            dve.wait_ge(loaded, 32)
            nc.vector.tensor_scalar_max(r1[:, :, :], b1_sb[:, :, :], 0.0).then_inc(made, 1)
            dve.wait_ge(used, E + 1)
            nc.vector.tensor_copy(row[:, :], row_ps[:, 0:D]).then_inc(made, 1)

        @block.tensor
        def _(pe):
            pe.wait_ge(made, 2)
            for e in range(E):
                pe.wait_ge(w2_in[e % 2], 16 * (e // 2 + 1))
                for c in range(KC):
                    last = nc.tensor.matmul(row_ps[:, 0:D], r1[:, e, c:c + 1], w2[e % 2][:, c, :],
                                            start=(e == 0 and c == 0), stop=False)
                last.then_inc(used, 1)
            nc.tensor.matmul(row_ps[:, 0:D], ones[:, :], b2_sb[:, :], start=False, stop=True).then_inc(used, 1)


def dispatch(nc, sem, xf_d, sort_d, xs_d):
    with ExitStack() as ctx:
        place = ctx.enter_context(nc.sbuf_tensor("d_place", [P, NT], I32))
        rows = [ctx.enter_context(nc.sbuf_tensor(f"d_rows{i}", [P, D], F32)) for i in range(4)]
        loaded = sem("d_loaded")
        row_in, sent = ([sem(f"d_{w}{i}") for i in range(4)] for w in ("row_in", "sent"))
        block = ctx.enter_context(nc.Block())

        @block.sync
        def _(sp):
            sp.dma_start(place[:, :], sort_d[:, :]).then_inc(loaded, 16)
            for t in range(NT):
                if t >= 4:
                    sp.wait_ge(sent[t % 4], 16 * (t // 4))
                sp.dma_start(rows[t % 4][:, :], xf_d[t * P:(t + 1) * P, :]).then_inc(row_in[t % 4], 16)

        @block.gpsimd
        def _(pool):
            pool.wait_ge(loaded, 16)
            for t in range(NT):
                pool.wait_ge(row_in[t % 4], 16 * (t // 4 + 1))
                nc.gpsimd.indirect_dma_start(xs_d[:, :], bass.IndirectOffsetOnAxis(ap=place[:, t:t + 1], axis=0),
                                             rows[t % 4][:, :], None).then_inc(sent[t % 4], 16)
            for i in range(4):
                pool.wait_ge(sent[i], 16 * (NT // 4))


def experts(nc, sem, W1, b1, W2, c_masks, expert_d, total_d, xs_d, ys_d):
    KC = HID // P
    BUFS = 4
    with ExitStack() as ctx:
        def sb(name, shape, dt=F32):
            return ctx.enter_context(nc.sbuf_tensor("e_" + name, shape, dt))

        def ps(name, shape):
            return ctx.enter_context(nc.psum_tensor("e_" + name, shape, F32))

        masks = sb("masks", [P, 5, P])
        total = sb("total", [1, D])
        expert = sb("expert", [1, ET], I32)
        w1 = [sb(f"w1_{i}", [P, 2, HID]) for i in range(BUFS)]
        w2 = [sb(f"w2_{i}", [P, KC, D]) for i in range(BUFS)]
        bias = [sb(f"bias{i}", [P, KC]) for i in range(BUFS)]
        xs = [sb(f"xs{i}", [P, D]) for i in range(BUFS)]
        low, off = sb("low", [P, 2, KC]), sb("off", [P, 2, KC])
        xT = sb("xT", [P, 2, 2, P])
        hid = sb("hid", [P, 2, KC, P])
        ys = sb("ys", [P, 2, D])
        turn_ps = ps("turn_ps", [P, 4, P])
        hid_ps = [ps(f"hid_ps{i}", [P, KC, P]) for i in range(2)]
        out_ps = [ps(f"out_ps{i}", [P, 512]) for i in range(2)]
        held = sem("e_held")
        loaded = sem("e_loaded")
        tile_in = [sem(f"e_tile_in{q}") for q in range(BUFS)]
        stored = [sem(f"e_stored{i}") for i in range(2)]
        turned, xT_made, hid_made, low_made, relu_made, out_made, ys_made = (
            sem("e_turned"), sem("e_xT"), sem("e_hid"), sem("e_low"), sem("e_relu"), sem("e_out"), sem("e_ys"))

        def hold(eng, semaphore, value):
            eng.wait_ge(semaphore, value)
            eng.sem_inc(held, 1)

        block = ctx.enter_context(nc.Block())

        def steps(eng, step):
            for q in range(BUFS):
                step(0, q)
            with eng.Fori(1, ET // BUFS) as k:
                for q in range(BUFS):
                    step(k, q)

        def below(k, q, count):
            return isinstance(k, int) and BUFS * k + q < count

        @block.sync
        def _(sp):
            sp.dma_start(masks[:, :, :], c_masks).then_inc(loaded, 16)
            sp.dma_start(total[:, :], total_d[:, :]).then_inc(loaded, 16)
            sp.dma_start(expert[:, :], expert_d[:, :]).then_inc(loaded, 16)
            hold(sp, loaded, 48)

            def load(k, q):
                s = k * BUFS + q
                if not below(k, q, BUFS):
                    hold(sp, out_made, s - 3)
                e = sp.value_load(expert[0:1, bass.ds(s, 1)], min_val=0, max_val=E - 1)
                sp.dma_start(xs[q][:, :], view(xs_d, s * (P * D), [[D, P], [1, D]])).then_inc(tile_in[q], 16)
                sp.dma_start(w1[q][:, :, :], view(W1.tensor, e * (D * HID), [[HID, P], [P * HID, 2], [1, HID]])
                             ).then_inc(tile_in[q], 16)
                sp.dma_start(w2[q][:, :, :], view(W2.tensor, e * (HID * D), [[D, P], [P * D, KC], [1, D]])
                             ).then_inc(tile_in[q], 16)
                sp.dma_start(bias[q][:, :], view(b1.tensor, e * HID, [[1, P], [P, KC]]),
                             allow_slow_non_contiguous=True).then_inc(tile_in[q], 16)
            steps(sp, load)

        @block.scalar
        def _(act):
            def store(k, q):
                s, i = k * BUFS + q, q % 2
                act.wait_ge(out_made, s + 1)
                if not below(k, q, 2):
                    act.wait_ge(stored[i], k * 32 + q // 2 * 16)
                nc.scalar.copy(ys[:, i, :], out_ps[i][:, 0:D]).then_inc(ys_made, 1)
                act.wait_ge(ys_made, s + 1)
                act.dma_start(view(ys_d, s * (P * D), [[D, P], [1, D]]), ys[:, i, :]).then_inc(stored[i], 16)

            def step(k, q):
                s, i = k * BUFS + q, q % 2
                act.wait_ge(turned, s + 1)
                if not below(k, q, 2):
                    act.wait_ge(hid_made, s - 1)
                nc.scalar.copy(xT[:, i, :, :], turn_ps[:, 2 * i:2 * i + 2, :]).then_inc(xT_made, 1)
                if not below(k, q, 2):
                    store(k, q - 2)
            steps(act, step)
            for q in (BUFS - 2, BUFS - 1):
                store(ET // BUFS - 1, q)
            for i in range(2):
                act.wait_ge(stored[i], 8 * ET)

        @block.vector
        def _(dve):
            def step(k, q):
                s, i = k * BUFS + q, q % 2
                dve.wait_ge(tile_in[q], k * 64 + 64)
                if not below(k, q, 2):
                    dve.wait_ge(relu_made, s - 1)
                nc.vector.tensor_scalar(off[:, i, :], bias[q][:, :], 0.0, -1.0, ALU.max, ALU.mult).then_inc(low_made, 1)
                nc.vector.tensor_scalar(low[:, i, :], bias[q][:, :], 0.0, None, ALU.min).then_inc(low_made, 1)
                dve.wait_ge(low_made, s * 2 + 2)
                dve.wait_ge(hid_made, s + 1)
                if not below(k, q, 2):
                    dve.wait_ge(out_made, s - 1)
                for c in range(KC):
                    last = nc.vector.tensor_scalar(hid[:, i, c, :], hid_ps[i][:, c, :], low[:, i, c:c + 1],
                                                   off[:, i, c:c + 1], ALU.add, ALU.max)
                last.then_inc(relu_made, 1)
            steps(dve, step)

        @block.tensor
        def _(pe):
            pe.wait_ge(loaded, 48)

            def second(k, q):
                s, i = k * BUFS + q, q % 2
                pe.wait_ge(relu_made, s + 1)
                if not below(k, q, 2):
                    pe.wait_ge(ys_made, s - 1)
                for c in range(KC):
                    nc.tensor.matmul(out_ps[i][:, 0:D], hid[:, i, c, :], w2[q % BUFS][:, c, :], start=(c == 0), stop=False)
                nc.tensor.matmul(out_ps[i][:, 0:D], masks[0:1, 3, :], total[:, :], start=False, stop=True).then_inc(out_made, 1)

            def step(k, q):
                s, i = k * BUFS + q, q % 2
                pe.wait_ge(tile_in[q], k * 64 + 64)
                if not below(k, q, 2):
                    pe.wait_ge(xT_made, s - 1)
                for f in range(2):
                    last = nc.tensor.transpose(turn_ps[:, 2 * i + f, :], xs[q][:, f * P:(f + 1) * P], masks[:, 4, :])
                last.then_inc(turned, 1)
                if not below(k, q, 2):
                    second(k, q - 2)
                pe.wait_ge(xT_made, s + 1)
                if not below(k, q, 2):
                    pe.wait_ge(relu_made, s - 1)
                for c in range(KC):
                    for f in range(2):
                        last = nc.tensor.matmul(hid_ps[i][:, c, :], w1[q][:, f, c * P:(c + 1) * P], xT[:, i, f, :],
                                                start=(f == 0), stop=(f == 1))
                last.then_inc(hid_made, 1)
            steps(pe, step)
            for q in (BUFS - 2, BUFS - 1):
                second(ET // BUFS - 1, q)


def finish(nc, sem, x2_d, sort_d, ys_d, out):
    with ExitStack() as ctx:
        def sb(name, shape, dt=F32):
            return ctx.enter_context(nc.sbuf_tensor("f_" + name, shape, dt))

        NB = 4
        place = sb("place", [P, NT], I32)
        y, x2, z = (sb(n, [P, NB, D]) for n in ("y", "x2", "z"))
        stats, mv, var, root, inv = (sb(n, [P, NB, k]) for n, k in
                                     (("stats", 6), ("mv", 2), ("var", 1), ("root", 1), ("inv", 1)))
        loaded = sem("f_loaded")
        y_in, x2_in, stored = ([sem(f"f_{w}{i}") for i in range(NB)] for w in ("y_in", "x2_in", "stored"))
        dve_s = Stages(sem("f_dve"), "stats", "mv", "var", "inv", "normal", "sum")
        rooted = sem("f_rooted")
        block = ctx.enter_context(nc.Block())

        @block.sync
        def _(sp):
            sp.dma_start(place[:, :], sort_d[:, :]).then_inc(loaded, 16)
            for t in range(NT):
                if t >= NB:
                    sp.wait_ge(dve_s.sem, dve_s.before(t - NB + 1))
                sp.dma_start(x2[:, t % NB, :], x2_d[t * P:(t + 1) * P, :]).then_inc(x2_in[t % NB], 16)

        @block.gpsimd
        def _(pool):
            pool.wait_ge(loaded, 16)
            for t in range(NT):
                if t >= NB:
                    pool.wait_ge(dve_s.sem, dve_s.before(t - NB + 1))
                nc.gpsimd.indirect_dma_start(y[:, t % NB, :], None, ys_d[:, :],
                                             bass.IndirectOffsetOnAxis(ap=place[:, t:t + 1], axis=0)).then_inc(y_in[t % NB], 16)

        @block.vector
        def _(dve):
            dve.sem_inc(dve_s.sem, 1)
            s = dve_s
            for t in range(NT):
                i = t % NB
                dve.wait_ge(y_in[i], 16 * (t // NB + 1))
                nc.vector.bn_stats(stats[:, i, :], y[:, i, :]).then_inc(s.sem, 1)
                dve.wait_ge(s.sem, s.after(t, "stats"))
                nc.vector.bn_aggr(mv[:, i, :], stats[:, i, :]).then_inc(s.sem, 1)
                dve.wait_ge(s.sem, s.after(t, "mv"))
                nc.vector.tensor_scalar_add(var[:, i, :], mv[:, i, 1:2], EPS).then_inc(s.sem, 1)
                dve.wait_ge(rooted, t + 1)
                nc.vector.reciprocal(inv[:, i, :], root[:, i, :]).then_inc(s.sem, 1)
                dve.wait_ge(s.sem, s.after(t, "inv"))
                if t >= NB:
                    dve.wait_ge(stored[i], 16 * (t // NB))
                nc.vector.tensor_scalar(z[:, i, :], y[:, i, :], mv[:, i, 0:1], inv[:, i, :], ALU.subtract, ALU.mult
                                        ).then_inc(s.sem, 1)
                dve.wait_ge(s.sem, s.after(t, "normal"))
                dve.wait_ge(x2_in[i], 16 * (t // NB + 1))
                nc.vector.tensor_tensor(z[:, i, :], z[:, i, :], x2[:, i, :], ALU.add).then_inc(s.sem, 1)

        @block.scalar
        def _(act):
            for t in range(NT):
                i = t % NB
                act.wait_ge(dve_s.sem, dve_s.after(t, "var"))
                nc.scalar.activation(root[:, i, :], var[:, i, :], ACT.Sqrt).then_inc(rooted, 1)
                act.wait_ge(dve_s.sem, dve_s.after(t, "sum"))
                act.dma_start(out[t * P:(t + 1) * P, :], z[:, i, :]).then_inc(stored[i], 16)
            for i in range(NB):
                act.wait_ge(stored[i], 16 * (NT // NB))


_INS = ['hidden_states', 'Wq', 'bq', 'Wk', 'bk', 'Wv', 'bv', 'Wo', 'bo', 'rel_embeddings', 'ln_scale', 'ln_bias']
_FFN = ['W1', 'b1', 'W2', 'b2', 'Wr', 'br']


def kernel(**inputs):
    import numpy as _np
    import concourse.bacc as _bacc
    from concourse import mybir as _mybir
    from concourse.bass_utils import run_bass_kernel_spmd as _run

    nc = _bacc.Bacc("TRN2", target_bir_lowering=False, num_devices=1)
    arrays, args = {}, []
    given = {"L0_attn_" + n: inputs["L0_attn_" + n] for n in _INS} | {"L0_ffn_" + n: inputs["L0_ffn_" + n] for n in _FFN}
    for name, value in (given | constants()).items():
        a = _np.ascontiguousarray(value)
        if name == "L0_attn_hidden_states":
            a = a.reshape(TOK, D)
        arrays[f"in_{name}_dram"] = a
        args.append(nc.dram_tensor(f"in_{name}_dram", a.shape, _mybir.dt.from_np(a.dtype), kind="ExternalInput").ap())
    args.append(nc.dram_tensor("out_0_dram", (TOK, D), F32, kind="ExternalOutput").ap())
    build(nc, *args)
    r = _run(nc, [arrays], core_ids=[0])
    return r.results[0]["out_0_dram"].reshape(B, S, D)
```
